# Optimizing a Trainium2 kernel written in Bass

```python
import numpy as np
import jax
import jax.numpy as jnp

def _softmax(x, axis=-1):
    return jax.nn.softmax(x, axis=axis)

def _gelu(x):
    return jax.nn.gelu(x, approximate=True)

def _silu(x):
    return jax.nn.silu(x)

def _sigmoid(x):
    return jax.nn.sigmoid(x)

def _layernorm(x, axis=-1, eps=1e-05):
    m = jnp.mean(x, axis=axis, keepdims=True)
    v = jnp.var(x, axis=axis, keepdims=True)
    return (x - m) / jnp.sqrt(v + eps)

def _scatter_add(tgt, idx, src, axis=0):
    return tgt.at[idx].add(src)

def _segment_sum(src, seg, n):
    return jax.ops.segment_sum(src, seg, n)
kernel_name = 'mk_adj_preln_d2_adj_r2_72ab54'

def setup_inputs(seed: int=0):
    np.random.seed(seed)
    _w = jnp.asarray

    def _rec_inputs():
        import jax
        import jax.numpy as jnp
        _gk = jax.random.key(seed)
        x = -0.0002928 + 1 * jax.random.normal(jax.random.fold_in(_gk, 1), (4096, 256), jnp.float32)
        _a = jax.random.bernoulli(jax.random.fold_in(_gk, 2), 0.00195312, (4096, 4096))
        adj = _a.astype(jnp.int32)
        return (x, adj)
    x, adj = _rec_inputs()

    def _L0_gnn_setup():
        import jax, jax.numpy as jnp
        import numpy as np
        N, D_IN, D_OUT = (4096, 256, 256)
        key = jax.random.key(seed)
        ks = jax.random.split(key, 8)
        scale_in = 1.0 / np.sqrt(D_IN)
        scale_cat = 1.0 / np.sqrt(2 * D_OUT)
        return {'x': jax.random.normal(ks[0], (N, D_IN), dtype=jnp.float32), 'adj': jax.random.randint(ks[1], (N, N), 0, 2, dtype=jnp.int32), 'W_self': jax.random.uniform(ks[2], (D_IN, D_OUT), jnp.float32, -scale_in, scale_in), 'b_self': jax.random.uniform(ks[3], (D_OUT,), jnp.float32, -scale_in, scale_in), 'W_nb': jax.random.uniform(ks[4], (D_IN, D_OUT), jnp.float32, -scale_in, scale_in), 'b_nb': jax.random.uniform(ks[5], (D_OUT,), jnp.float32, -scale_in, scale_in), 'W_comb': jax.random.uniform(ks[6], (2 * D_OUT, D_OUT), jnp.float32, -scale_cat, scale_cat), 'b_comb': jax.random.uniform(ks[7], (D_OUT,), jnp.float32, -scale_cat, scale_cat)}
    _L0_gnn_all = _L0_gnn_setup()
    _L0_gnn_in = {k: v for k, v in _L0_gnn_all.items() if k in ('W_self', 'b_self', 'W_nb', 'b_nb', 'W_comb', 'b_comb')}
    del _L0_gnn_all

    def _L1_gnn_setup():
        import jax, jax.numpy as jnp
        import numpy as np
        NEG_SLOPE = 0.2
        N, IN_DIM, OUT_DIM, N_HEADS = (2048, 256, 256, 4)
        D_K = OUT_DIM // N_HEADS
        key = jax.random.key(seed)
        k1, k2, k3, k4, k5 = jax.random.split(key, 5)
        H = jax.random.normal(k1, (N, IN_DIM), dtype=jnp.float32)
        A = jax.random.randint(k2, (N, N), 0, 2, dtype=jnp.int32)
        W = jax.random.normal(k3, (IN_DIM, OUT_DIM), dtype=jnp.float32) * (1.0 / np.sqrt(IN_DIM))
        a_l = jax.random.normal(k4, (N_HEADS, D_K), dtype=jnp.float32) * 0.1
        a_r = jax.random.normal(k5, (N_HEADS, D_K), dtype=jnp.float32) * 0.1
        return {'H': H, 'A': A, 'W': W, 'a_l': a_l, 'a_r': a_r}
    _L1_gnn_all = _L1_gnn_setup()
    _L1_gnn_in = {k: v for k, v in _L1_gnn_all.items() if k in ('W', 'a_l', 'a_r')}
    del _L1_gnn_all
    return {'x': x, 'adj': adj, 'L0_gnn_W_self': _L0_gnn_in['W_self'], 'L0_gnn_b_self': _L0_gnn_in['b_self'], 'L0_gnn_W_nb': _L0_gnn_in['W_nb'], 'L0_gnn_b_nb': _L0_gnn_in['b_nb'], 'L0_gnn_W_comb': _L0_gnn_in['W_comb'], 'L0_gnn_b_comb': _L0_gnn_in['b_comb'], 'L1_gnn_W': _L1_gnn_in['W'], 'L1_gnn_a_l': _L1_gnn_in['a_l'], 'L1_gnn_a_r': _L1_gnn_in['a_r']}

def reference(x, adj, L0_gnn_W_self, L0_gnn_b_self, L0_gnn_W_nb, L0_gnn_b_nb, L0_gnn_W_comb, L0_gnn_b_comb, L1_gnn_W, L1_gnn_a_l, L1_gnn_a_r):
    import jax
    import jax.numpy as jnp

    def _L0_gnn_ref(x, adj, W_self, b_self, W_nb, b_nb, W_comb, b_comb):
        import jax, jax.numpy as jnp
        import numpy as np
        N, D_IN, D_OUT = (4096, 256, 256)
        mask = (adj > 0).astype(x.dtype)
        deg = jnp.sum(mask, axis=1, keepdims=True)
        agg = mask @ x / jnp.maximum(deg, 1.0)
        self_f = x @ W_self + b_self
        nb_f = agg @ W_nb + b_nb
        combined = jnp.concatenate([self_f, nb_f], axis=-1)
        out = combined @ W_comb + b_comb
        return jax.nn.relu(out)

    def _L1_gnn_ref(H, A, W, a_l, a_r):
        import jax, jax.numpy as jnp
        import numpy as np
        NEG_SLOPE = 0.2
        N, IN_DIM, OUT_DIM, N_HEADS = (2048, 256, 256, 4)
        D_K = OUT_DIM // N_HEADS
        n = H.shape[0]
        mask = A + jnp.eye(n, dtype=A.dtype) > 0
        Wh = (H @ W).reshape(n, N_HEADS, D_K)
        sl = jnp.einsum('nhd,hd->nh', Wh, a_l)
        sr = jnp.einsum('nhd,hd->nh', Wh, a_r)
        e = jax.nn.leaky_relu(sl[:, :, None] + sr.T[None, :, :], negative_slope=NEG_SLOPE)
        e = jnp.where(mask[:, None, :], e, -jnp.inf)
        alpha = jnp.nan_to_num(jax.nn.softmax(e, axis=2), nan=0.0)
        out = jnp.einsum('nhm,mhd->nhd', alpha, Wh).reshape(n, OUT_DIM)
        return jax.nn.elu(out)
    h = jnp.maximum(_layernorm(x, axis=-1), 0.0)
    x = x + _L0_gnn_ref(h, adj, L0_gnn_W_self, L0_gnn_b_self, L0_gnn_W_nb, L0_gnn_b_nb, L0_gnn_W_comb, L0_gnn_b_comb)
    h = jnp.maximum(_layernorm(x, axis=-1), 0.0)
    x = x + _L1_gnn_ref(h, adj, L1_gnn_W, L1_gnn_a_l, L1_gnn_a_r)
    return x

_drawn_inputs = setup_inputs


def setup_inputs(seed=0):
    import zlib

    import numpy as np

    out = dict(_drawn_inputs(seed))
    spreads = {}
    factors = {'L0_gnn_b_self': 5.646, 'L0_gnn_b_nb': 5.091, 'L0_gnn_b_comb': 3.1, 'L1_gnn_a_l': 3.606}
    for name, (base, spread) in spreads.items():
        noise = np.random.default_rng([zlib.crc32(name.encode()), seed]).standard_normal(out[name].shape)
        drawn = base * np.exp(spread * noise) if base else spread * noise
        out[name] = jnp.asarray(drawn.astype(out[name].dtype))
    for name, factor in factors.items():
        out[name] = (out[name] * factor).astype(out[name].dtype)
    return out
```

```python
from contextlib import ExitStack

import concourse.bass as bass
from concourse import mybir

F32 = mybir.dt.float32
F16 = mybir.dt.float16
BF16 = mybir.dt.bfloat16
F8 = mybir.dt.float8e4
I32 = mybir.dt.int32
I8 = mybir.dt.int8
U8 = mybir.dt.uint8
U16 = mybir.dt.uint16
ALU = mybir.AluOpType
ACT = mybir.ActivationFunctionType
AX_X = mybir.AxisListType.X

P = 128
N = 4096
D = 256
H = 4
DK = D // H
NK = N // (2 * P)
NT = 2 * NK
ONE = 0x38
GSCALE = 16.0
VSCALE = 256.0
EPS = 1e-5
SLOPE = 0.2
DV = DK + 1
STRIP = 1024
NS = N // STRIP
NJ = STRIP // P
NG = H * NS
VBLK = 2 * DV
CH = 4
NCH = NK // CH
VSTEPS = 6


def build(nc, x, adj, W_self, b_self, W_nb, b_nb, W_comb, b_comb, W, a_l, a_r, out):
    own_d = nc.dram_tensor("own_scratch", (NK, P, 2 * D), F32, kind="Internal").ap()
    x1_d = nc.dram_tensor("x1_scratch", (NT, P, D), F32, kind="Internal").ap()
    wh_d = nc.dram_tensor("wh_scratch", (NT, P, D), F32, kind="Internal").ap()
    s_d = nc.dram_tensor("s_scratch", (NG, STRIP), F32, kind="Internal").ap()

    with ExitStack() as ctx:
        def sb(name, shape, dt):
            return ctx.enter_context(nc.sbuf_tensor(name, shape, dt))

        def sem(name):
            return ctx.enter_context(nc.semaphore(name))

        mask = sb("mask", [P, NK, N], U16)
        wext = sb("wext", [P, 2, D + 2 * H], F32)
        ident = sb("ident", [P, P], F32)
        identb = sb("identb", [P, P], BF16)
        eps = sb("eps", [P, 1], F32)
        sr = sb("sr", [P, NT, 2 * H], F32)
        diag = sb("diag", [P, 2 * P], U16)
        mask32 = mask[:, :, :].bitcast(I32)

        ctx01 = ctx.enter_context(ExitStack())
        g = ctx01.enter_context(nc.sbuf_tensor("g", [P, NT, 2 * D], F16))
        phase0(nc, x, W_self, b_self, W_nb, b_nb, W_comb, b_comb, W, a_l, a_r,
               own_d, wext, ident, identb, eps, diag, g)
        phase1(nc, x, adj, own_d, x1_d, wh_d, mask, mask32, wext, ident, identb, eps, sr, g)
        ctx01.close()
        with ExitStack() as ctx23:
            fac = ctx23.enter_context(nc.sbuf_tensor("fac", [P, 4, H, NT], F32))
            rbias = ctx23.enter_context(nc.sbuf_tensor("rbias", [P, 2, NG, NT], F32))
            phase2(nc, mask32, sr, diag, ident, fac, rbias, s_d)
            phase3(nc, x1_d, wh_d, s_d, mask32, fac, rbias, out)


def phase0(nc, x, W_self, b_self, W_nb, b_nb, W_comb, b_comb, W, a_l, a_r,
           own_d, wext, ident, identb, eps, diag, g):
    x_v = x.rearrange("(k p e) d -> k p (e d)", p=P, e=2)
    with ExitStack() as ctx:
        def sb(name, shape, dt):
            return ctx.enter_context(nc.sbuf_tensor(name, shape, dt))

        def psum(name, shape, dt):
            return ctx.enter_context(nc.psum_tensor(name, shape, dt))

        def sem(name):
            return ctx.enter_context(nc.semaphore(name))

        w_in = sb("w_in", [P, 2, 2, D], F32)
        wc = sb("wc", [P, 4, D], F32)
        bcol = sb("bcol", [P, 4], F32)
        bwide = sb("bwide", [P, 4, P], F32)
        bcomb = sb("bcomb", [P, 1, D], F32)
        abc = sb("abc", [P, 2, 1, D], F32)
        aprod = sb("aprod", [P, D], F32)
        wT = sb("wT", [P, 4, D], F32)
        ab = sb("ab", [P, 2, 2 * D], F32)
        cbias = sb("cbias", [P, D], F32)
        diagf = sb("diagf", [P, 2, P], F32)
        xin = sb("xin", [P, 2, 2 * D], F32)
        stats = sb("stats", [P, 2, 6], F32)
        mv = sb("mv", [P, 2, 2], F32)
        std = sb("std", [P, 2], F32)
        rstd = sb("rstd", [P, 2], F32)
        shift = sb("shift", [P, 2], F32)
        h = sb("h", [P, 2, 2 * D], F32)
        hT = sb("hT", [P, 2, 4 * P], F32)
        own = sb("own", [P, 2, 2 * D], F32)
        ps_w = psum("ps_w", [P, 512], F32)
        ps_b = psum("ps_b", [P, 512], F32)
        ps_hT = [psum(f"ps_hT{i}", [P, 4 * P], F32) for i in range(2)]
        ps_mm = [psum(f"ps_mm{i}", [P, 2 * D], F32) for i in range(4)]

        waits_passed = sem("waits_passed0")
        weights_in = sem("weights_in")
        zeroed = sem("zeroed")
        consts = sem("consts")
        wT_ready = sem("wT_ready")
        wT_copied = sem("wT_copied")
        bwide_ready = sem("bwide_ready")
        wmm_ready = sem("wmm_ready")
        ab_ready = sem("ab_ready")
        wa_step = sem("wa_step")
        x_in = [sem(f"x_in{i}") for i in range(2)]
        dve_step = sem("dve_step")
        var_ready = sem("var_ready")
        std_ready = sem("std_ready")
        norm_ready = sem("norm_ready")
        h_ready = sem("h_ready")
        hT_ready = sem("hT_ready")
        hT_copied = sem("hT_copied")
        mm_ready = sem("mm_ready")
        high_ready = sem("high_ready")
        own_ready = sem("own_ready")
        mm_free = sem("mm_free")
        own_out = [sem(f"own_out{i}") for i in range(2)]
        block = ctx.enter_context(nc.Block())

        @block.sync
        def _(sp):
            sp.dma_start(xin[:, 0, :], x_v[0]).then_inc(x_in[0], 16)
            sp.dma_start(xin[:, 1, :], x_v[1]).then_inc(x_in[1], 16)
            with nc.allow_non_contiguous_dma(reason="bias vectors as columns, 256 elements each"):
                for i, b in enumerate((b_self, b_nb)):
                    sp.dma_start(bcol[:, 2 * i:2 * i + 2],
                                 b.rearrange("(c p) -> p c", p=P)).then_inc(weights_in, 16)
            for i, w in enumerate((W_self, W_nb)):
                sp.dma_start(w_in[:, i, :, :], w.rearrange("(c p) d -> p c d", p=P)).then_inc(weights_in, 16)
            sp.dma_start(wc[:, :, :], W_comb.rearrange("(c p) d -> p c d", p=P)).then_inc(weights_in, 16)
            sp.dma_start(wext[:, :, 0:D], W.rearrange("(c p) d -> p c d", p=P)).then_inc(weights_in, 16)
            sp.dma_start(bcomb[:, :, :], b_comb.rearrange("(a d) -> a d", a=1).partition_broadcast(P)
                         ).then_inc(weights_in, 16)
            for i, a in enumerate((a_l, a_r)):
                sp.dma_start(abc[:, i, :, :], a.rearrange("(o h) d -> o (h d)", o=1).partition_broadcast(P)
                             ).then_inc(weights_in, 16)
            with sp.Fori(0, NK // 2 - 1) as i:
                for b in range(2):
                    sp.wait_ge(h_ready, i * 2 + b + 1)
                    sp.dma_start(xin[:, b, :], x_v[bass.ds(i * 2 + (b + 2), 1)].rearrange("o p d -> p (o d)")
                                 ).then_inc(x_in[b], 16)

        @block.gpsimd
        def _(pool):
            nc.gpsimd.memset(ident[:, :], 0.0).then_inc(zeroed, 1)
            nc.gpsimd.memset(diagf[:, :, :], 0.0).then_inc(zeroed, 1)
            nc.gpsimd.memset(eps[:, :], EPS).then_inc(consts, 1)
            pool.wait_ge(zeroed, 2)
            nc.gpsimd.affine_select(out=ident[:, :], in_=ident[:, :], compare_op=ALU.not_equal, fill=1.0,
                                    base=0, pattern=[[-1, P]], channel_multiplier=1).then_inc(consts, 1)
            for e in range(2):
                nc.gpsimd.affine_select(out=diagf[:, e, :], in_=diagf[:, e, :], compare_op=ALU.not_equal,
                                        fill=float(ONE << (8 * e)), base=0, pattern=[[-1, P]],
                                        channel_multiplier=1).then_inc(consts, 1)
            pool.wait_ge(consts, 4)
            nc.gpsimd.tensor_copy(identb[:, :], ident[:, :]).then_inc(consts, 1)
            nc.gpsimd.tensor_copy(diag[:, :], diagf[:, :, :].rearrange("p e n -> p (e n)")).then_inc(consts, 1)
            with pool.Fori(0, NK // 2) as i:
                for b in range(2):
                    pool.wait_ge(own_ready, (i * 2 + b) * 2 + 2)
                    pool.dma_start(own_d[bass.ds(i * 2 + b, 1)].rearrange("o p d -> p (o d)"),
                                   own[:, b, :]).then_inc(own_out[b], 16)
            for b in range(2):
                pool.wait_ge(own_out[b], 16 * (NK // 2))

        @block.tensor
        def _(pe):
            pe.wait_ge(weights_in, 16 * 9)
            pe.wait_ge(consts, 4)
            for i in range(2):
                if i:
                    pe.wait_ge(wT_copied, 1)
                for c in range(2):
                    for q in range(2):
                        last = nc.tensor.transpose(ps_w[:, (q * 2 + c) * P:(q * 2 + c + 1) * P],
                                                   w_in[:, i, c, q * P:(q + 1) * P], ident[:, :])
                last.then_inc(wT_ready, 1)
            pe.wait_ge(wT_copied, 2)
            for c in range(2):
                for i in range(2):
                    for q in range(2):
                        last = nc.tensor.matmul(ps_mm[c][:, i * D:(i + 1) * D],
                                                wT[:, 2 * i + q, c * P:(c + 1) * P], wc[:, 2 * i + q, :],
                                                start=(i == 0 and q == 0), stop=(q == 1),
                                                skip_group_check=True)
                last.then_inc(wmm_ready, 1)
            pe.wait_ge(bwide_ready, 1)
            for q in range(4):
                last = nc.tensor.matmul(ps_b[:, 0:D], bwide[:, q, :], wc[:, q, :], start=(q == 0), stop=(q == 3))
            last.then_inc(wmm_ready, 1)

            def transposes(k, b):
                pe.wait_ge(h_ready, k + 1)
                pe.wait_ge(hT_copied, k + 1)
                for q in range(4):
                    last = nc.tensor.transpose(ps_hT[b][:, q * P:(q + 1) * P],
                                               h[:, b, q * P:(q + 1) * P], ident[:, :])
                last.then_inc(hT_ready, 1)

            def products(k, b):
                pe.wait_ge(hT_copied, k + 3)
                pe.wait_ge(mm_free, 2 * k + 2)
                for e in range(2):
                    for c in range(2):
                        last = nc.tensor.matmul(ps_mm[2 * b + e][:, :],
                                                hT[:, b, (2 * e + c) * P:(2 * e + c + 1) * P], ab[:, c, :],
                                                start=(c == 0), stop=(c == 1))
                    last.then_inc(mm_ready, 1)

            transposes(0, 0)
            pe.wait_ge(ab_ready, 3)
            with pe.Fori(0, NK // 2 - 1) as i:
                for b in range(2):
                    transposes(i * 2 + (b + 1), 1 - b)
                    products(i * 2 + b, b)
            transposes(NK - 1, 1)
            products(NK - 2, 0)
            products(NK - 1, 1)

        @block.scalar
        def _(act):
            act.sem_inc(hT_copied, 2)
            for i in range(2):
                act.wait_ge(wT_ready, i + 1)
                nc.scalar.activation(wT[:, 2 * i:2 * i + 2, :].rearrange("p q d -> p (q d)"), ps_w[:, :],
                                     ACT.Copy).then_inc(wT_copied, 1)
            for c in range(2):
                act.wait_ge(wmm_ready, c + 1)
                nc.scalar.activation(ab[:, c, 0:D], ps_mm[c][:, 0:D], ACT.Copy)
                nc.scalar.activation(ab[:, c, D:2 * D], ps_mm[c][:, D:2 * D], ACT.Copy, scale=GSCALE
                                     ).then_inc(ab_ready, 1)
            act.wait_ge(consts, 4)

            def norm(k, b):
                act.wait_ge(var_ready, k + 1)
                nc.scalar.activation(std[:, :], mv[:, :, 1], ACT.Sqrt, bias=eps[:, 0:1]).then_inc(std_ready, 1)
                act.wait_ge(norm_ready, k + 1)
                for e in range(2):
                    last = nc.scalar.activation(h[:, b, e * D:(e + 1) * D], xin[:, b, e * D:(e + 1) * D], ACT.Relu,
                                                bias=shift[:, e:e + 1], scale=rstd[:, e:e + 1])
                last.then_inc(h_ready, 1)
                act.wait_ge(hT_ready, k + 1)
                nc.scalar.activation(hT[:, b, :], ps_hT[b][:, :], ACT.Copy).then_inc(hT_copied, 1)

            def highs(k, b):
                for e in range(2):
                    act.wait_ge(mm_ready, k * 2 + (e + 1))
                    nc.scalar.activation(g[:, bass.ds(k * 2 + e, 1), 0:D], ps_mm[2 * b + e][:, D:2 * D].unsqueeze(1),
                                         ACT.Copy).then_inc(high_ready, 1)

            norm(0, 0)
            with act.Fori(0, NK // 2 - 1) as i:
                for b in range(2):
                    norm(i * 2 + (b + 1), 1 - b)
                    highs(i * 2 + b, b)
            norm(NK - 1, 1)
            highs(NK - 2, 0)
            highs(NK - 1, 1)

        @block.vector
        def _(dve):
            dve.sem_inc(mm_free, 4)
            dve.wait_ge(weights_in, 16 * 9)
            nc.vector.tensor_copy(bwide[:, :, :], bcol[:, :].unsqueeze(2).to_broadcast([P, 4, P])
                                  ).then_inc(bwide_ready, 1)
            n = 0
            for c in range(2):
                for i in range(2):
                    nc.vector.tensor_tensor(aprod[:, :], wext[:, c, 0:D], abc[:, i, 0, :], ALU.mult
                                            ).then_inc(wa_step, 1)
                    n += 1
                    dve.wait_ge(wa_step, n)
                    nc.vector.tensor_reduce(wext[:, c, D + H * i:D + H * (i + 1)],
                                            aprod[:, :].rearrange("p (h d) -> p h d", h=H), AX_X, ALU.add
                                            ).then_inc(wa_step, 1)
                    n += 1
                    dve.wait_ge(wa_step, n)

            def norm(k, b, i):
                dve.wait_ge(x_in[b], (i + 1) * 16)
                for e in range(2):
                    last = nc.vector.bn_stats(stats[:, e, :], xin[:, b, e * D:(e + 1) * D])
                last.then_inc(dve_step, 1)
                dve.wait_ge(dve_step, k * 2 + 1)
                dve.wait_ge(h_ready, k)
                hold(dve, waits_passed)
                for e in range(2):
                    last = nc.vector.bn_aggr(mv[:, e, :], stats[:, e, :])
                last.then_inc(var_ready, 1)
                dve.wait_ge(std_ready, k + 1)
                nc.vector.reciprocal(rstd[:, :], std[:, :]).then_inc(dve_step, 1)
                dve.wait_ge(dve_step, k * 2 + 2)
                nc.vector.scalar_tensor_tensor(shift[:, :], mv[:, :, 0], -1.0, rstd[:, :], ALU.mult, ALU.mult
                                               ).then_inc(norm_ready, 1)

            def outputs(k, b, i):
                if not isinstance(i, int) or i:
                    dve.wait_ge(own_out[b], i * 16)
                for e in range(2):
                    bank = ps_mm[2 * b + e]
                    dve.wait_ge(high_ready, k * 2 + (e + 1))
                    nc.vector.tensor_tensor(own[:, b, e * D:(e + 1) * D], bank[:, 0:D], cbias[:, :], ALU.add
                                            ).then_inc(own_ready, 1)
                    nc.vector.tensor_tensor(g[:, bass.ds(k * 2 + e, 1), D:2 * D], bank[:, D:2 * D].unsqueeze(1),
                                            g[:, bass.ds(k * 2 + e, 1), 0:D], ALU.subtract).then_inc(mm_free, 1)

            norm(0, 0, 0)
            dve.wait_ge(wmm_ready, 3)
            nc.vector.tensor_tensor(cbias[:, :], ps_b[:, 0:D], bcomb[:, 0, :], ALU.add).then_inc(ab_ready, 1)
            dve.wait_ge(ab_ready, 3)
            def two_pairs(i):
                norm(i * 2 + 1, 1, i)
                outputs(i * 2, 0, i)
                norm(i * 2 + 2, 0, i + 1)
                outputs(i * 2 + 1, 1, i)

            two_pairs(0)
            with dve.Fori(1, NK // 2 - 1) as i:
                two_pairs(i)
            norm(NK - 1, 1, NK // 2 - 1)
            outputs(NK - 2, 0, NK // 2 - 1)
            outputs(NK - 1, 1, NK // 2 - 1)


def phase1(nc, x, adj, own_d, x1_d, wh_d, mask, mask32, wext, ident, identb, eps, sr, g):
    x_v = x.rearrange("(k p e) d -> k p (e d)", p=P, e=2)
    adj_v = adj.rearrange("(k p e) m -> k p (e m)", p=P, e=2)
    HALF = N // 2
    HK = NK // 2
    with ExitStack() as ctx:
        def sb(name, shape, dt):
            return ctx.enter_context(nc.sbuf_tensor(name, shape, dt))

        def psum(name, shape, dt):
            return ctx.enter_context(nc.psum_tensor(name, shape, dt))

        def sem(name):
            return ctx.enter_context(nc.semaphore(name))

        stage = sb("stage", [P, 2, HALF], I32)
        bits = sb("bits", [P, 2, HALF], U8)
        junk = sb("junk", [P, HALF], U8)
        degp = sb("degp", [P, NT, 2], F32)
        mT = sb("mT", [P, 2, N // 2], BF16)
        own = sb("own1", [P, 2, D], F32)
        xt = sb("xt", [P, 2, D], F32)
        deg = sb("deg", [P, 3], F32)
        part = sb("part", [P, D], F32)
        x1 = sb("x1", [P, 2, D], F32)
        stats = sb("stats1", [P, 6], F32)
        mv = sb("mv1", [P, 2], F32)
        std = sb("std1", [P, 1], F32)
        rstd = sb("rstd1", [P, 1], F32)
        shift = sb("shift1", [P, 1], F32)
        h1 = sb("h1", [P, 2, D], F32)
        h1T = sb("h1T", [P, 2, D], F32)
        wh = sb("wh", [P, 2, D], F32)
        ps_t = [psum(f"ps_t{i}", [P, HK * P], BF16) for i in range(2)]
        ps_a = [psum(f"ps_a{i}", [P, 2 * D], F32) for i in range(2)]
        ps_h = psum("ps_h", [P, D], F32)
        ps_w = psum("ps_wh", [P, D + 2 * H], F32)

        waits_passed = sem("waits_passed1")
        stage_in = [sem(f"stage_in{i}") for i in range(2)]
        row_in = [sem(f"row_in{i}") for i in range(2)]
        bits_ready = sem("bits_ready")
        deg_ready = sem("deg_ready")
        words_ready = sem("words_ready")
        words_copied = sem("words_copied")
        kept = sem("kept")
        agg_ready = sem("agg_ready")
        post_step = sem("post_step")
        x1_ready = sem("x1_ready")
        var_ready = sem("var1_ready")
        std_ready = sem("std1_ready")
        norm_ready = sem("norm1_ready")
        h1_ready = sem("h1_ready")
        h1T_ready = sem("h1T_ready")
        h1T_copied = sem("h1T_copied")
        wmm_ready = sem("wh_mm_ready")
        wh_ready = sem("wh_ready")
        sr_ready = sem("sr_ready")
        x1_out = [sem(f"x1_out{i}") for i in range(2)]
        wh_out = [sem(f"wh_out{i}") for i in range(2)]
        block = ctx.enter_context(nc.Block())

        @block.sync
        def _(sp):
            def rows(k, e):
                for f in range(2):
                    if not (isinstance(k, int) and k == 0 and e == 0):
                        sp.wait_ge(bits_ready, (k * 2 + e) * 2 - 1 + f)
                    sp.dma_start(stage[:, f, :],
                                 adj_v[bass.ds(k, 1), :, e * N + f * HALF:e * N + (f + 1) * HALF]
                                 .rearrange("o p m -> p (o m)")).then_inc(stage_in[f], 16)

            for e in range(2):
                rows(0, e)
            with sp.Fori(1, NK) as k:
                for e in range(2):
                    rows(k, e)

        @block.gpsimd
        def _(pool):
            def keep(k, e):
                for f in range(2):
                    pool.wait_ge(words_copied, (k * 2 + e) * 2 + (f + 1))
                    hold(pool, waits_passed)
                    nc.gpsimd.tensor_copy(
                        mask32[:, f * HK:(f + 1) * HK, bass.ds((k * 2 + e) * (P // 2), P // 2)],
                        mT[:, e, f * HK * P:(f + 1) * HK * P].bitcast(I32).rearrange("p (k n) -> p k n", k=HK)
                    ).then_inc(kept, 1)

            def row(k, e):
                for dst, src in ((xt, x_v), (own, own_d)):
                    pool.dma_start(dst[:, e, :], src[bass.ds(k, 1), :, e * D:(e + 1) * D]
                                   .rearrange("o p d -> p (o d)")).then_inc(row_in[e], 16)

            def store_x1(k, e):
                pool.wait_ge(x1_ready, k * 2 + (e + 1))
                pool.dma_start(x1_d[bass.ds(k * 2 + e, 1)].rearrange("o p d -> p (o d)"), x1[:, e, :]
                               ).then_inc(x1_out[e], 16)

            def store_wh(t, e):
                pool.wait_ge(wh_ready, t + 1)
                pool.dma_start(wh_d[bass.ds(t, 1)].rearrange("o p d -> p (o d)"), wh[:, e, :]
                               ).then_inc(wh_out[e], 16)

            row(0, 0)
            row(0, 1)
            keep(0, 0)
            keep(0, 1)
            store_x1(0, 0)
            row(1, 0)
            with pool.Fori(1, NK - 1) as k:
                keep(k, 0)
                store_x1(k - 1, 1)
                row(k, 1)
                store_wh(k * 2 - 2, 0)
                keep(k, 1)
                store_x1(k, 0)
                row(k + 1, 0)
                store_wh(k * 2 - 1, 1)
            keep(NK - 1, 0)
            store_x1(NK - 2, 1)
            row(NK - 1, 1)
            store_wh(NT - 4, 0)
            keep(NK - 1, 1)
            store_x1(NK - 1, 0)
            store_wh(NT - 3, 1)
            store_x1(NK - 1, 1)
            store_wh(NT - 2, 0)
            store_wh(NT - 1, 1)
            for e in range(2):
                pool.wait_ge(x1_out[e], 16 * NK)
                pool.wait_ge(wh_out[e], 16 * NK)

        @block.tensor
        def _(pe):
            def words(t, e):
                for f in range(2):
                    pe.wait_ge(bits_ready, t * 2 + (f + 1))
                    if not isinstance(t, int) or t >= 1:
                        pe.wait_ge(words_copied, t * 2 + (f - 1))
                    w = bits[:, f, :].bitcast(BF16)
                    for q in range(HK):
                        last = nc.tensor.transpose(ps_t[f][:, q * P:(q + 1) * P], w[:, q * P:(q + 1) * P],
                                                   identb[:, :])
                    last.then_inc(words_ready, 1)

            def sums(t, e, f):
                if f == 0:
                    pe.wait_ge(words_copied, t * 2 + 2)
                    if not isinstance(t, int) or t >= 2:
                        pe.wait_ge(x1_ready, t - 1)
                    hold(pe, waits_passed)
                m = mT[:, e, :].bitcast(F8).rearrange("p (k n b) -> p k b n", k=NK, b=2)
                for kk in range(f * HK, (f + 1) * HK):
                    for b in range(2):
                        last = nc.tensor.matmul(ps_a[e][:, :], m[:, kk, b, :], g[:, 2 * kk + b, :],
                                                start=(kk == 0 and b == 0), stop=(kk == NK - 1 and b == 1))
                if f == 1:
                    last.then_inc(agg_ready, 1)

            def turn_h1(t, e):
                pe.wait_ge(h1_ready, t + 1)
                if not isinstance(t, int) or t >= 1:
                    pe.wait_ge(h1T_copied, t)
                for c in range(2):
                    last = nc.tensor.transpose(ps_h[:, c * P:(c + 1) * P], h1[:, e, c * P:(c + 1) * P], ident[:, :])
                last.then_inc(h1T_ready, 1)

            def wh_product(t, e):
                pe.wait_ge(h1T_copied, t + 1)
                if not isinstance(t, int) or t >= 1:
                    pe.wait_ge(sr_ready, t)
                for c in range(2):
                    last = nc.tensor.matmul(ps_w[:, :], h1T[:, e, c * P:(c + 1) * P], wext[:, c, :],
                                            start=(c == 0), stop=(c == 1))
                last.then_inc(wmm_ready, 1)

            def tile(t, e, first=False, final=False):
                sums(t, e, 0)
                if not final:
                    words(t + 1, 1 - e)
                if not first:
                    turn_h1(t - 1, 1 - e)
                sums(t, e, 1)
                if not first:
                    wh_product(t - 1, 1 - e)

            words(0, 0)
            tile(0, 0, first=True)
            tile(1, 1)
            with pe.Fori(1, NK - 1) as k:
                for e in range(2):
                    tile(k * 2 + e, e)
            tile(NT - 2, 0)
            tile(NT - 1, 1, final=True)
            turn_h1(NT - 1, 1)
            wh_product(NT - 1, 1)

        @block.vector
        def _(dve):
            def to_bits(t):
                for f in range(2):
                    dve.wait_ge(stage_in[f], (t + 1) * 16)
                    if not (isinstance(t, int) and t == 0):
                        dve.wait_ge(words_ready, t * 2 + (f - 1))
                        dve.wait_ge(deg_ready, t * 2 + (f - 1))
                    nc.vector.tensor_scalar(bits[:, f, :], stage[:, f, :], 0.0, float(ONE), ALU.is_gt, ALU.mult
                                            ).then_inc(bits_ready, 1)

            def copy_words(t, e):
                for f in range(2):
                    dve.wait_ge(words_ready, t * 2 + (f + 1))
                    if not isinstance(t, int) or t >= 2:
                        if f == 0:
                            dve.wait_ge(agg_ready, t - 1)
                        dve.wait_ge(kept, t * 2 + (f - 3))
                    nc.vector.tensor_copy(mT[:, e, f * HK * P:(f + 1) * HK * P], ps_t[f][:, :]
                                          ).then_inc(words_copied, 1)

            def post(t, e, k):
                STEPS = 7

                def link(ins, n):
                    ins.then_inc(post_step, 1)
                    dve.wait_ge(post_step, t * STEPS + n)

                dve.wait_ge(deg_ready, t * 2 + 2)
                link(nc.vector.tensor_reduce(deg[:, 0:1], degp[:, bass.ds(t, 1), :], AX_X, ALU.add), 1)
                link(nc.vector.tensor_scalar(deg[:, 1:2], deg[:, 0:1], float(ONE), GSCALE / ONE, ALU.max, ALU.mult), 2)
                link(nc.vector.reciprocal(deg[:, 2:3], deg[:, 1:2]), 3)
                dve.wait_ge(agg_ready, t + 1)
                dve.wait_ge(row_in[e], (k + 1) * 32)
                link(nc.vector.scalar_tensor_tensor(part[:, :], ps_a[e][:, 0:D], deg[:, 2:3], own[:, e, :],
                                                    ALU.mult, ALU.add), 4)
                link(nc.vector.scalar_tensor_tensor(part[:, :], ps_a[e][:, D:2 * D], deg[:, 2:3], part[:, :],
                                                    ALU.mult, ALU.add), 5)
                if not isinstance(t, int) or t >= 2:
                    dve.wait_ge(x1_out[e], k * 16)
                    dve.wait_ge(h1_ready, t - 1)
                nc.vector.scalar_tensor_tensor(x1[:, e, :], part[:, :], 0.0, xt[:, e, :], ALU.max, ALU.add
                                               ).then_inc(x1_ready, 1)
                dve.wait_ge(x1_ready, t + 1)
                link(nc.vector.bn_stats(stats[:, :], x1[:, e, :]), 6)
                if not isinstance(t, int) or t >= 1:
                    dve.wait_ge(h1_ready, t)
                hold(dve, waits_passed)
                nc.vector.bn_aggr(mv[:, :], stats[:, :]).then_inc(var_ready, 1)
                dve.wait_ge(std_ready, t + 1)
                link(nc.vector.reciprocal(rstd[:, :], std[:, :]), 7)
                nc.vector.scalar_tensor_tensor(shift[:, :], mv[:, 0:1], -1.0, rstd[:, :], ALU.mult, ALU.mult
                                               ).then_inc(norm_ready, 1)

            to_bits(0)
            copy_words(0, 0)
            to_bits(1)
            copy_words(1, 1)
            to_bits(2)
            post(0, 0, 0)
            copy_words(2, 0)
            to_bits(3)
            post(1, 1, 0)
            with dve.Fori(1, NK - 1) as k:
                for e in range(2):
                    copy_words(k * 2 + (e + 1), 1 - e)
                    to_bits(k * 2 + (e + 2))
                    post(k * 2 + e, e, k)
            copy_words(NT - 1, 1)
            post(NT - 2, 0, NK - 1)
            post(NT - 1, 1, NK - 1)

        @block.scalar
        def _(act):
            def degrees(t):
                for f in range(2):
                    act.wait_ge(deg_ready, t * 2 + f)
                    act.wait_ge(bits_ready, t * 2 + (f + 1))
                    nc.scalar.activation(junk[:, :], bits[:, f, :], ACT.Copy,
                                         accum_out=degp[:, bass.ds(t, 1), f:f + 1].rearrange("p o f -> p (o f)")
                                         ).then_inc(deg_ready, 1)

            def norm(t, e):
                act.wait_ge(var_ready, t + 1)
                nc.scalar.activation(std[:, :], mv[:, 1:2], ACT.Sqrt, bias=eps[:, 0:1]).then_inc(std_ready, 1)
                act.wait_ge(norm_ready, t + 1)
                if not isinstance(t, int) or t >= 2:
                    act.wait_ge(h1T_ready, t - 1)
                nc.scalar.activation(h1[:, e, :], x1[:, e, :], ACT.Relu, bias=shift[:, 0:1], scale=rstd[:, 0:1]
                                     ).then_inc(h1_ready, 1)

            def copy_h1T(t, e):
                act.wait_ge(h1T_ready, t + 1)
                nc.scalar.activation(h1T[:, e, :], ps_h[:, :], ACT.Copy).then_inc(h1T_copied, 1)

            def copy_wh(t, e, k):
                act.wait_ge(wmm_ready, t + 1)
                if not isinstance(k, int) or k:
                    act.wait_ge(wh_out[e], k * 16)
                nc.scalar.activation(wh[:, e, :], ps_w[:, 0:D], ACT.Copy, scale=VSCALE).then_inc(wh_ready, 1)
                nc.scalar.activation(sr[:, bass.ds(t, 1), :], ps_w[:, D:D + 2 * H].unsqueeze(1), ACT.Copy
                                     ).then_inc(sr_ready, 1)

            degrees(0)
            degrees(1)
            degrees(2)
            norm(0, 0)
            copy_h1T(0, 0)
            copy_wh(0, 0, 0)
            degrees(3)
            norm(1, 1)
            def two_tiles(k):
                copy_h1T(k * 2 - 1, 1)
                copy_wh(k * 2 - 1, 1, k - 1)
                degrees(k * 2 + 2)
                norm(k * 2, 0)
                copy_h1T(k * 2, 0)
                copy_wh(k * 2, 0, k)
                degrees(k * 2 + 3)
                norm(k * 2 + 1, 1)

            two_tiles(1)
            with act.Fori(2, NK - 1) as k:
                two_tiles(k)
            copy_h1T(NT - 3, 1)
            copy_wh(NT - 3, 1, NK - 2)
            norm(NT - 2, 0)
            copy_h1T(NT - 2, 0)
            copy_wh(NT - 2, 0, NK - 1)
            norm(NT - 1, 1)
            copy_h1T(NT - 1, 1)
            copy_wh(NT - 1, 1, NK - 1)


def phase2(nc, mask32, sr, diag, ident, fac, rbias, s_d):
    with ExitStack() as ctx:
        def sb(name, shape, dt):
            return ctx.enter_context(nc.sbuf_tensor(name, shape, dt))

        def sem(name):
            return ctx.enter_context(nc.semaphore(name))

        rmax = sb("rmax", [P, H], F32)
        rall = sb("rall", [P, H], F32)
        s_c = sb("s_c", [P, H, NT], F32)
        r_c = sb("r_c", [P, H, NT], F32)
        dr = sb("dr", [P, H, NT], F32)
        y = sb("y", [P, H, NT], F32)
        bound = sb("bound", [P, H, NT], F32)
        ex = sb("ex", [P, 2, H, NT], F32)
        s_row = sb("s_row", [P, P], F32)
        ps_s = ctx.enter_context(nc.psum_tensor("ps_s", [P, P], F32))
        rmax_ready = sem("rmax_ready")
        rall_ready = sem("rall_ready")
        s_compact = sem("s_compact")
        sT_ready = sem("sT_ready")
        s_row_ready = sem("s_row_ready")
        s_out = sem("s_out")
        step = sem("step2")
        expo_ready = sem("expo_ready")
        done = sem("done2")
        block = ctx.enter_context(nc.Block())

        @block.vector
        def _(dve):
            n = 0

            def link(ins):
                nonlocal n
                n += 1
                ins.then_inc(step, 1)
                dve.wait_ge(step, n)

            nc.vector.tensor_reduce(rmax[:, :], sr[:, :, H:2 * H].rearrange("p t h -> p h t"), AX_X, ALU.max
                                    ).then_inc(rmax_ready, 1)
            nc.vector.tensor_copy(s_c[:, :, :], sr[:, :, 0:H].rearrange("p t h -> p h t")).then_inc(s_compact, 1)
            link(nc.vector.tensor_copy(r_c[:, :, :], sr[:, :, H:2 * H].rearrange("p t h -> p h t")))
            dve.wait_ge(rall_ready, 1)
            dve.wait_ge(s_compact, 1)
            for h in range(H):
                nc.vector.tensor_scalar(dr[:, h, :], r_c[:, h, :], rall[:, h:h + 1], None, ALU.subtract)
                last = nc.vector.tensor_scalar(y[:, h, :], s_c[:, h, :], rall[:, h:h + 1], None, ALU.add)
            link(last)
            last = nc.vector.scalar_tensor_tensor(bound[:, :, :], y[:, :, :], SLOPE, y[:, :, :], ALU.mult, ALU.max)
            link(last)
            nc.vector.tensor_tensor(ex[:, 0, :, :], y[:, :, :], bound[:, :, :], ALU.subtract)
            nc.vector.scalar_tensor_tensor(ex[:, 1, :, :], y[:, :, :], SLOPE, bound[:, :, :], ALU.mult,
                                           ALU.subtract).then_inc(expo_ready, 1)
            for h in range(H):
                for i, sign in enumerate((1.0, -1.0)):
                    nc.vector.tensor_scalar(rbias[:, i, h * NS:(h + 1) * NS, :],
                                            r_c[:, h, :].unsqueeze(1).to_broadcast([P, NS, NT]),
                                            sign, None, ALU.mult)
            for k in range(NK):
                blk = mask32[:, k, k * P:(k + 1) * P]
                last = nc.vector.tensor_tensor(blk, blk, diag[:, :].bitcast(I32), ALU.bitwise_or)
            last.then_inc(done, 1)

        @block.gpsimd
        def _(pool):
            pool.wait_ge(rmax_ready, 1)
            nc.gpsimd.partition_all_reduce(rall[:, :], rmax[:, :], P, bass.bass_isa.ReduceOp.max
                                           ).then_inc(rall_ready, 1)

        @block.tensor
        def _(pe):
            pe.wait_ge(s_compact, 1)
            nc.tensor.transpose(ps_s[:, :], s_c[:, :, :].rearrange("p h t -> p (h t)"), ident[:, :]
                                ).then_inc(sT_ready, 1)

        @block.scalar
        def _(act):
            act.wait_ge(sT_ready, 1)
            nc.scalar.activation(s_row[:, :], ps_s[:, :], ACT.Copy).then_inc(s_row_ready, 1)
            act.wait_ge(expo_ready, 1)
            nc.scalar.activation(fac[:, 0, :, :], dr[:, :, :], ACT.Exp)
            nc.scalar.activation(fac[:, 1, :, :], dr[:, :, :], ACT.Exp, scale=SLOPE)
            nc.scalar.activation(fac[:, 2:4, :, :], ex[:, :, :, :], ACT.Exp).then_inc(done, 1)

        @block.sync
        def _(sp):
            sp.wait_ge(s_row_ready, 1)
            sp.dma_start(s_d.rearrange("g (j p) -> (g j) p", p=P), s_row[:, :]).then_inc(s_out, 16)
            sp.wait_ge(s_out, 16)
            sp.wait_ge(done, 2)


def phase3(nc, x1_d, wh_d, s_d, mask32, fac, rbias, out):
    x1_v = x1_d.rearrange("(s j) p (h d) -> s h p j d", j=NJ, h=H)
    wh_v = wh_d.rearrange("t p (h d) -> h p t d", h=H)
    out_v = out.rearrange("(s k p e) (h d) -> s h e p k d", s=NS, p=P, e=2, h=H)
    WS = STRIP // 2
    ASIGN = NK + NK // 2
    with ExitStack() as ctx:
        def sb(name, shape, dt):
            return ctx.enter_context(nc.sbuf_tensor(name, shape, dt))

        def sem(name):
            return ctx.enter_context(nc.semaphore(name))

        srow = sb("srow", [P, 2, 1, STRIP], F32)
        sgn = sb("sgn", [P, 2, 2 * STRIP], I8)
        pos = sb("pos", [P, 4, WS], I32)
        neg = sb("neg", [P, 4, WS], I32)
        val = sb("val", [P, NT, 2 * VBLK], F16)
        whx = sb("whx", [P, NT, DV], F32)
        vtmp = sb("vtmp", [P, 2 * CH, DV], F32)
        total = sb("total", [P, NJ, VBLK], F32)
        num = sb("num", [P, NJ, DV], F32)
        den = sb("den", [P, 2, NJ], F32)
        y = sb("yout", [P, NJ, DK], F32)
        ylow = sb("ylow", [P, NJ, DK], F32)
        x1s = sb("x1s", [P, NJ, DK], F32)
        acc = [ctx.enter_context(nc.psum_tensor(f"acc{j}", [P, 512], F32)) for j in range(NJ)]

        waits_passed = sem("waits_passed3")
        ones_set = sem("ones_set")
        s_in = sem("s_in")
        wh_in = sem("wh_in")
        x1_in = sem("x1_in")
        act_signs = sem("act_signs")
        dve_signs = sem("dve_signs")
        neg_ready = sem("neg_ready")
        split_ready = sem("split_ready")
        pe_block = sem("pe_block")
        pe_bank = sem("pe_bank")
        val_step = sem("val_step")
        minus_ready = sem("minus_ready")
        plus_ready = sem("plus_ready")
        num_ready = sem("num_ready")
        den_step = sem("den_step")
        den_ready = sem("den_ready")
        y_step = sem("y_step")
        ylow_ready = sem("ylow_ready")
        exp_ready = sem("exp_ready")
        y_ready = sem("y_ready")
        stored = sem("stored")
        block = ctx.enter_context(nc.Block())

        @block.sync
        def _(sp):
            def load_s(gr, slot):
                sp.dma_start(srow[:, bass.ds(slot, 1), :, :].rearrange("p a o n -> p (a o) n"),
                             s_d[bass.ds(gr, 1), :].partition_broadcast(P)).then_inc(s_in, 16)

            def load_x1(gr):
                sp.dma_start(x1s[:, :, :], x1_v[bass.ds(gr % NS, 1), bass.ds(gr // NS, 1)]
                             .rearrange("a b p j d -> p (a b j) d")).then_inc(x1_in, 16)

            def store(gr):
                sp.wait_ge(y_ready, gr + 1)
                for e in range(2):
                    sp.dma_start(out_v[bass.ds(gr % NS, 1), bass.ds(gr // NS, 1), e]
                                 .rearrange("a b p k d -> p (a b k) d"),
                                 y[:, :, :].rearrange("p (k e) d -> p e k d", e=2)[:, e]).then_inc(stored, 16)

            def next_s(gr):
                sp.wait_ge(act_signs, (gr + 1) * ASIGN)
                hold(sp, waits_passed)
                sp.wait_ge(dve_signs, (gr + 1) * (NT - ASIGN))
                sp.wait_ge(s_in, (gr + 2) * 16)
                load_s(gr + 2, gr % 2)

            sp.sem_inc(stored, 32)
            load_s(0, 0)
            sp.wait_ge(s_in, 16)
            load_s(1, 1)
            load_x1(0)
            next_s(0)
            with sp.Fori(1, NG - 2) as gr:
                store(gr - 1)
                load_x1(gr)
                next_s(gr)
            for gr in (NG - 2, NG - 1):
                store(gr - 1)
                load_x1(gr)
            store(NG - 1)
            sp.wait_ge(stored, 32 * (NG + 1))

        @block.tensor
        def _(pe):
            def bytes_of(t):
                return t.bitcast(F8).rearrange("p (n b) -> p b n", b=2)

            with pe.Fori(0, NG) as gr:
                for k in range(NK):
                    if k % CH == 0:
                        pe.wait_ge(val_step, gr // NS * (NCH * VSTEPS) + (k // CH + 1) * VSTEPS)
                    pe.wait_ge(split_ready, gr * NK + (k + 1))
                    hold(pe, waits_passed)
                    for j in range(NJ):
                        if k == 0:
                            pe.wait_ge(minus_ready, gr * NJ + (j + 1))
                            pe.wait_ge(plus_ready, gr * NJ + (j + 1))
                            hold(pe, waits_passed)
                        for b in range(2):
                            first = k == 0 and b == 0
                            final = k == NK - 1 and b == 1
                            for br, m in enumerate((pos, neg)):
                                last = nc.tensor.matmul(
                                    acc[j][:, br * VBLK:(br + 1) * VBLK],
                                    bytes_of(m[:, k % 4, j * (P // 2):(j + 1) * (P // 2)])[:, b, :],
                                    val[:, 2 * k + b, br * VBLK:(br + 1) * VBLK],
                                    start=first and br == 0, stop=final, skip_group_check=True)
                        if k == NK - 1:
                            last.then_inc(pe_bank, 1)
                    if k < NK - 1:
                        last.then_inc(pe_block, 1)

        @block.scalar
        def _(act):
            act.sem_inc(minus_ready, NJ)

            def sign(gr, k, b):
                if not (isinstance(gr, int) and k < 2):
                    act.wait_ge(neg_ready, gr * NK + (k - 1))
                nc.scalar.activation(sign_bytes(sgn, k, b), srow[:, bass.ds(gr % 2, 1), 0, :].rearrange("p o n -> p (o n)"),
                                     ACT.Sign, bias=rbias[:, 0, bass.ds(gr, 1), 2 * k + b]).then_inc(act_signs, 1)

            def read_minus(gr):
                for j in range(NJ):
                    act.wait_ge(pe_bank, gr * NJ + (j + 1))
                    if j == 0:
                        act.wait_ge(num_ready, gr + 1)
                    nc.scalar.activation(total[:, j, :], acc[j][:, VBLK:2 * VBLK], ACT.Copy,
                                         scale=fac_col(fac, 3, gr, j)).then_inc(minus_ready, 1)

            def group(gr, first):
                act.wait_ge(s_in, (gr + 1) * 16)
                for k in range(NK):
                    for b in range(2):
                        if not dve_has(k, b):
                            sign(gr, k, b)
                    if k == 1 and not first:
                        read_minus(gr - 1)
                    if k == 6 and not first:
                        act.wait_ge(ylow_ready, gr)
                        nc.scalar.activation(ylow[:, :, :], ylow[:, :, :], ACT.Exp).then_inc(exp_ready, 1)

            group(0, True)
            with act.Fori(1, NG) as gr:
                group(gr, False)
            read_minus(NG - 1)
            act.wait_ge(ylow_ready, NG)
            nc.scalar.activation(ylow[:, :, :], ylow[:, :, :], ACT.Exp).then_inc(exp_ready, 1)

        @block.vector
        def _(dve):
            dve.sem_inc(plus_ready, NJ)

            def split(gr, k, first):
                if dve_has(k, 1):
                    nc.vector.tensor_scalar(sign_bytes(sgn, k, 1),
                                            srow[:, bass.ds(gr % 2, 1), 0, :].rearrange("p o n -> p (o n)"),
                                            rbias[:, 1, bass.ds(gr, 1), 2 * k + 1], float(ONE), ALU.is_lt, ALU.mult
                                            ).then_inc(dve_signs, 1)
                    dve.wait_ge(dve_signs, gr * (NT - ASIGN) + sum(dve_has(q, 1) for q in range(k + 1)))
                dve.wait_ge(act_signs, gr * ASIGN + sum(not dve_has(q, b) for q in range(k + 1) for b in range(2)))
                if not (first and k < 4):
                    if k >= 4:
                        dve.wait_ge(pe_block, gr * (NK - 1) + (k - 3))
                    elif k < 3:
                        dve.wait_ge(pe_block, gr * (NK - 1) + (k - 2))
                    else:
                        dve.wait_ge(pe_bank, gr * NJ)
                m = mask32[:, k, bass.ds((gr % NS) * WS, WS)]
                sg = sgn[:, k % 2, :].bitcast(I32)
                nc.vector.tensor_tensor(neg[:, k % 4, :], sg, m, ALU.bitwise_and).then_inc(neg_ready, 1)
                dve.wait_ge(neg_ready, gr * NK + (k + 1))
                nc.vector.tensor_tensor(pos[:, k % 4, :], neg[:, k % 4, :], m, ALU.bitwise_xor
                                        ).then_inc(split_ready, 1)

            def read_plus(gr):
                for j in range(NJ):
                    dve.wait_ge(minus_ready, gr * NJ + (NJ + j + 1))
                    nc.vector.scalar_tensor_tensor(total[:, j, :], acc[j][:, 0:VBLK], fac_col(fac, 2, gr, j),
                                                   total[:, j, :], ALU.mult, ALU.add).then_inc(plus_ready, 1)

            def denominators(gr):
                dve.wait_ge(num_ready, gr + 2)
                nc.vector.tensor_scalar(den[:, 0, :], num[:, :, DK], 1e-30, None, ALU.max).then_inc(den_step, 1)
                dve.wait_ge(den_step, gr + 1)
                nc.vector.reciprocal(den[:, 1, :], den[:, 0, :]).then_inc(den_ready, 1)

            def group(gr, first):
                dve.wait_ge(s_in, (gr + 1) * 16)
                for k in range(NK):
                    split(gr, k, first)
                    if k == 1 and not first:
                        read_plus(gr - 1)
                    if k == 4 and not first:
                        denominators(gr - 1)

            group(0, True)
            with dve.Fori(1, NG) as gr:
                group(gr, False)
            read_plus(NG - 1)
            denominators(NG - 1)

        @block.gpsimd
        def _(pool):
            def load_wh(h):
                pool.dma_start(whx[:, :, 0:DK], wh_v[bass.ds(h, 1)].rearrange("o p t d -> p (o t) d")
                               ).then_inc(wh_in, 16)

            pool.sem_inc(num_ready, 1)
            load_wh(0)
            nc.gpsimd.memset(whx[:, :, DK:DV], VSCALE).then_inc(ones_set, 1)
            pool.wait_ge(ones_set, 1)

            def values(h, first):
                pool.wait_ge(wh_in, (h + 1) * 16)
                for c in range(NCH):
                    if not first:
                        if c < NCH - 1:
                            pool.wait_ge(pe_block, (h * NS - 1) * (NK - 1) + (c + 1) * CH)
                        else:
                            pool.wait_ge(pe_bank, h * NS * NJ)
                    t0 = 2 * CH * c
                    for br in range(2):
                        n = (h * NCH + c) * VSTEPS + 3 * br
                        hi = val[:, t0:t0 + 2 * CH, br * VBLK:br * VBLK + DV]
                        lo = val[:, t0:t0 + 2 * CH, br * VBLK + DV:(br + 1) * VBLK]
                        f = fac[:, br, bass.ds(h, 1), t0:t0 + 2 * CH].rearrange("p o t -> p (o t)")
                        pool.wait_ge(val_step, n)
                        nc.gpsimd.tensor_tensor(vtmp[:, :, :], whx[:, t0:t0 + 2 * CH, :],
                                                f.unsqueeze(2).to_broadcast([P, 2 * CH, DV]), ALU.mult
                                                ).then_inc(val_step, 1)
                        pool.wait_ge(val_step, n + 1)
                        hold(pool, waits_passed)
                        nc.gpsimd.tensor_copy(hi, vtmp[:, :, :]).then_inc(val_step, 1)
                        pool.wait_ge(val_step, n + 2)
                        nc.gpsimd.tensor_tensor(lo, vtmp[:, :, :], hi, ALU.subtract).then_inc(val_step, 1)

            def finish(gr):
                YS = 3
                pool.wait_ge(plus_ready, gr * NJ + 2 * NJ)
                nc.gpsimd.tensor_tensor(num[:, :, :], total[:, :, 0:DV], total[:, :, DV:VBLK], ALU.add
                                        ).then_inc(num_ready, 1)
                pool.wait_ge(den_ready, gr + 1)
                pool.wait_ge(stored, (gr + 1) * 32)
                nc.gpsimd.tensor_tensor(y[:, :, :], num[:, :, 0:DK],
                                        den[:, 1, :].unsqueeze(2).to_broadcast([P, NJ, DK]), ALU.mult
                                        ).then_inc(y_step, 1)
                pool.wait_ge(y_step, gr * YS + 1)
                hold(pool, waits_passed)
                nc.gpsimd.tensor_scalar(ylow[:, :, :], y[:, :, :], 0.0, None, ALU.min).then_inc(ylow_ready, 1)
                pool.wait_ge(ylow_ready, gr + 1)
                hold(pool, waits_passed)
                nc.gpsimd.tensor_scalar(y[:, :, :], y[:, :, :], 0.0, -1.0, ALU.max, ALU.add).then_inc(y_step, 1)
                pool.wait_ge(y_step, gr * YS + 2)
                pool.wait_ge(exp_ready, gr + 1)
                nc.gpsimd.tensor_tensor(y[:, :, :], y[:, :, :], ylow[:, :, :], ALU.add).then_inc(y_step, 1)
                pool.wait_ge(y_step, gr * YS + 3)
                pool.wait_ge(x1_in, (gr + 1) * 16)
                nc.gpsimd.tensor_tensor(y[:, :, :], y[:, :, :], x1s[:, :, :], ALU.add).then_inc(y_ready, 1)

            values(0, True)
            with pool.Fori(0, H - 1) as h:
                pool.wait_ge(val_step, (h + 1) * (NCH * VSTEPS))
                load_wh(h + 1)
                with pool.Fori(0, NS - 1) as s:
                    finish(h * NS + s)
                values(h + 1, False)
                finish(h * NS + (NS - 1))
            with pool.Fori(0, NS) as s:
                finish(s + (H - 1) * NS)


def hold(eng, waits_passed):
    eng.sem_inc(waits_passed, 1)


def dve_has(k, b):
    return b == 1 and k % 2 == 1


def sign_bytes(sgn, k, b):
    return sgn[:, k % 2, :].rearrange("p (n b) -> p b n", b=2)[:, b, :]


def fac_col(fac, i, gr, j):
    return fac[:, i, :, :].rearrange("p h t -> p (h t)")[:, bass.ds(gr * NJ + j, 1)]


_INS = ["x", "adj", "L0_gnn_W_self", "L0_gnn_b_self", "L0_gnn_W_nb", "L0_gnn_b_nb", "L0_gnn_W_comb",
        "L0_gnn_b_comb", "L1_gnn_W", "L1_gnn_a_l", "L1_gnn_a_r"]


def kernel(**inputs):
    import numpy as _np
    import concourse.bacc as _bacc
    from concourse import mybir as _mybir
    from concourse.bass_utils import run_bass_kernel_spmd as _run

    nc = _bacc.Bacc("TRN2", target_bir_lowering=False, num_devices=1)
    arrays, args = {}, []
    for name in _INS:
        a = _np.ascontiguousarray(inputs[name])
        arrays[f"in_{name}"] = a
        args.append(nc.dram_tensor(f"in_{name}", a.shape, _mybir.dt.from_np(a.dtype), kind="ExternalInput").ap())
    out = nc.dram_tensor("out", (N, D), F32, kind="ExternalOutput").ap()
    build(nc, *args, out)
    r = _run(nc, [arrays], core_ids=[0])
    return r.results[0]["out"]
```

```python
from contextlib import ExitStack

import concourse.bass as bass
from concourse import mybir

F32 = mybir.dt.float32
F16 = mybir.dt.float16
BF16 = mybir.dt.bfloat16
F8 = mybir.dt.float8e4
I32 = mybir.dt.int32
I8 = mybir.dt.int8
U8 = mybir.dt.uint8
U16 = mybir.dt.uint16
ALU = mybir.AluOpType
ACT = mybir.ActivationFunctionType
AX_X = mybir.AxisListType.X

P = 128
N = 4096
D = 256
H = 4
DK = D // H
NK = N // (2 * P)
NT = 2 * NK
ONE = 0x38
WSCALE = 256.0
GSCALE = 16.0
VSCALE = 256.0
EPS = 1e-5
SLOPE = 0.2
DV = DK + 1
STRIP = 1024
NS = N // STRIP
NJ = STRIP // P
NG = H * NS
VBLK = 2 * DV
CH = 4
NCH = NK // CH
NQ = NK // 2
VSTEPS = 6


def build(nc, x, adj, W_self, b_self, W_nb, b_nb, W_comb, b_comb, W, a_l, a_r, out):
    own_d = nc.dram_tensor("own_scratch", (NK, P, 2 * D), F32, kind="Internal").ap()
    x1_d = nc.dram_tensor("x1_scratch", (NT, P, D), F32, kind="Internal").ap()
    wh_d = nc.dram_tensor("wh_scratch", (NT, P, D), F32, kind="Internal").ap()
    s_d = nc.dram_tensor("s_scratch", (NG, STRIP), F32, kind="Internal").ap()
    s0_d = nc.dram_tensor("s0_scratch", (1, STRIP), F32, kind="Internal").ap()
    with ExitStack() as ctx:
        mask = ctx.enter_context(nc.sbuf_tensor("mask", [P, NK, N], U16))
        sr = ctx.enter_context(nc.sbuf_tensor("sr", [P, NT, 2 * H], F32))
        diag = ctx.enter_context(nc.sbuf_tensor("diag", [P, 2 * P], U16))
        ident = ctx.enter_context(nc.sbuf_tensor("ident", [P, P], F32))
        mask32 = mask[:, :, :].bitcast(I32)
        layer0(nc, x, adj, W_self, b_self, W_nb, b_nb, W_comb, b_comb, W, a_l, a_r,
               own_d, x1_d, wh_d, s0_d, mask, mask32, sr, diag, ident)
        layer1(nc, x1_d, wh_d, s_d, s0_d, mask32, sr, diag, ident, out)


def layer0(nc, x, adj, W_self, b_self, W_nb, b_nb, W_comb, b_comb, W, a_l, a_r,
           own_d, x1_d, wh_d, s0_d, mask, mask32, sr, diag, ident):
    x_v = x.rearrange("(k p e) d -> k p (e d)", p=P, e=2)
    adj_v = adj.rearrange("(k p e) m -> k p (e m)", p=P, e=2)
    HALF = N // 2
    HK = NK // 2
    NP2 = NK // 2
    E1 = D + 2 * H
    with ExitStack() as ctx:
        def sb(name, shape, dt):
            return ctx.enter_context(nc.sbuf_tensor(name, shape, dt))

        def psum(name, shape, dt):
            return ctx.enter_context(nc.psum_tensor(name, shape, dt))

        def sem(name):
            return ctx.enter_context(nc.semaphore(name))

        def early(k, at, n):
            return mask[:, k, N // 2 + 2 * at:N // 2 + 2 * (at + n)].bitcast(F32)

        g = sb("g", [P, NT, 2 * D], F16)
        identb = sb("identb", [P, P], BF16)
        eps = sb("eps", [P, 1], F32)
        w_in = [early(i, 0, 2 * D).rearrange("p (c d) -> p c d", c=2) for i in (0, 1)]
        wT = [early(i, 2 * D, 2 * D).rearrange("p (q d) -> p q d", q=2) for i in (0, 1)]
        wc = early(2, 0, 4 * D).rearrange("p (c d) -> p c d", c=4)
        bwide = early(3, 0, 4 * P).rearrange("p (c n) -> p c n", c=4)
        bcomb = early(3, 4 * P, D)
        cbias = early(3, 4 * P + D, D)
        w_raw = early(4, 0, 2 * E1).rearrange("p (c n) -> p c n", c=2)
        aprod = early(4, 2 * E1, D)
        abc = early(5, 0, 2 * D).rearrange("p (i d) -> p i d", i=2)
        diagf = early(5, 2 * D, 2 * P).rearrange("p (e n) -> p e n", e=2)
        bcol = early(5, 2 * D + 2 * P, 4)
        xin = early(6, 0, 4 * D).rearrange("p (b d) -> p b d", b=2)
        h = early(7, 0, 4 * D).rearrange("p (b d) -> p b d", b=2)
        ownA = early(8, 0, 4 * D).rearrange("p (b d) -> p b d", b=2)
        hT = [early(9 + i, 0, 2 * D).bitcast(F16).rearrange("p (b d) -> p b d", b=2) for i in (0, 1)]
        ab = [early(11 + i, 0, 2 * D).bitcast(F16).rearrange("p (c d) -> p c d", c=2) for i in (0, 1)]
        stats = early(13, 0, 12).rearrange("p (e n) -> p e n", e=2)
        mv = early(13, 16, 4).rearrange("p (e n) -> p e n", e=2)
        std = early(13, 32, 2)
        rstd = early(13, 48, 2)
        shift = early(13, 64, 2)
        wext = sb("wext", [P, 2, 2, E1], F16)
        stage = sb("stage", [P, 2, HALF], I32)
        bits = sb("bits", [P, 2, HALF], U8)
        junk = sb("junk", [P, HALF], U8)
        degp = sb("degp", [P, NT, 2], F32)
        mT = sb("mT", [P, 2, N // 2], BF16)
        own = sb("own", [P, 2, D], F32)
        xt = sb("xt", [P, 2, D], F32)
        deg = sb("deg", [P, 3], F32)
        part = sb("part", [P, D], F32)
        x1 = sb("x1", [P, 2, D], F32)
        stats1 = sb("stats1", [P, 6], F32)
        mv1 = sb("mv1", [P, 2], F32)
        std1 = sb("std1", [P, 1], F32)
        rstd1 = sb("rstd1", [P, 1], F32)
        shift1 = sb("shift1", [P, 1], F32)
        h1 = sb("h1", [P, 2, D], F32)
        h1T = sb("h1T", [P, 2, 2, D], F16)
        wh = sb("wh", [P, 2, D], F32)
        ps_t = [psum(f"ps_t{i}", [P, HK * P], BF16) for i in range(2)]
        ps_a = [psum(f"ps_a{i}", [P, 2 * D], F32) for i in range(2)]
        ps_x = [psum(f"ps_x{i}", [P, 2 * D], F32) for i in range(2)]
        ps_h = psum("ps_h", [P, 2 * D], F32)
        ps_w = psum("ps_w", [P, 2 * D], F32)
        ps_t32 = [t[:, :].bitcast(F32) for t in ps_t]
        ps_mm = ps_x + ps_a
        ps_hT = [ps_h, ps_w]

        waits_passed = sem("waits_passed")
        weights_in = sem("weights_in")
        zeroed = sem("zeroed")
        consts = sem("consts")
        wT_ready = sem("wT_ready")
        wT_copied = sem("wT_copied")
        bwide_ready = sem("bwide_ready")
        wmm_ready = sem("wmm_ready")
        ab_high = sem("ab_high")
        ab_ready = sem("ab_ready")
        wa_step = sem("wa_step")
        x_in = [sem(f"x_in{i}") for i in range(2)]
        dve_step = sem("dve_step")
        var_ready = sem("var_ready")
        std_ready = sem("std_ready")
        norm_ready = sem("norm_ready")
        h_ready = sem("h_ready")
        hT_ready = sem("hT_ready")
        hT_high = sem("hT_high")
        hT_copied = sem("hT_copied")
        mm_ready = sem("mm_ready")
        high_ready = sem("high_ready")
        own_ready = sem("own_ready")
        mm_free = sem("mm_free")
        own_out = [sem(f"own_out{i}") for i in range(2)]

        stage_in = [sem(f"stage_in{i}") for i in range(2)]
        row_in = [sem(f"row_in{i}") for i in range(2)]
        bits_ready = sem("bits_ready")
        deg_ready = sem("deg_ready")
        words_ready = sem("words_ready")
        words_copied = sem("words_copied")
        kept = sem("kept")
        agg_ready = sem("agg_ready")
        post_step = sem("post_step")
        x1_ready = sem("x1_ready")
        var1_ready = sem("var1_ready")
        std1_ready = sem("std1_ready")
        norm1_ready = sem("norm1_ready")
        h1_ready = sem("h1_ready")
        h1T_ready = sem("h1T_ready")
        h1T_high = sem("h1T_high")
        h1T_copied = sem("h1T_copied")
        wh_mm_ready = sem("wh_mm_ready")
        wh_ready = sem("wh_ready")
        sr_ready = sem("sr_ready")
        x1_out = [sem(f"x1_out{i}") for i in range(2)]
        wh_out = [sem(f"wh_out{i}") for i in range(2)]
        late_out = sem("late_out")
        block = ctx.enter_context(nc.Block())

        @block.sync
        def _(sp):
            sp.dma_start(xin[:, 0, :], x_v[0]).then_inc(x_in[0], 16)
            for i, w in enumerate((W_self, W_nb)):
                sp.dma_start(w_in[i], w.rearrange("(c p) d -> p c d", p=P)).then_inc(weights_in, 16)
            sp.dma_start(wc, W_comb.rearrange("(c p) d -> p c d", p=P)).then_inc(weights_in, 16)
            sp.dma_start(xin[:, 1, :], x_v[1]).then_inc(x_in[1], 16)
            with nc.allow_non_contiguous_dma(reason="bias vectors as columns, 256 elements each"):
                for i, b in enumerate((b_self, b_nb)):
                    sp.dma_start(bcol[:, 2 * i:2 * i + 2], b.rearrange("(c p) -> p c", p=P)
                                 ).then_inc(weights_in, 16)
            sp.dma_start(w_raw[:, :, 0:D], W.rearrange("(c p) d -> p c d", p=P)).then_inc(weights_in, 16)
            sp.dma_start(bcomb, b_comb.rearrange("(a d) -> a d", a=1).partition_broadcast(P)
                         .rearrange("p a d -> p (a d)")).then_inc(weights_in, 16)
            for i, a in enumerate((a_l, a_r)):
                sp.dma_start(abc[:, i, :], a.rearrange("(o h) d -> o (h d)", o=1).partition_broadcast(P)
                             .rearrange("p a d -> p (a d)")).then_inc(weights_in, 16)

            def rows(k, e):
                for f in range(2):
                    if not (isinstance(k, int) and k == 0 and e == 0):
                        sp.wait_ge(bits_ready, (k * 2 + e) * 2 - 1 + f)
                    sp.dma_start(stage[:, f, :],
                                 adj_v[bass.ds(k, 1), :, e * N + f * HALF:e * N + (f + 1) * HALF]
                                 .rearrange("o p m -> p (o m)")).then_inc(stage_in[f], 16)

            rows(0, 0)
            with sp.Fori(0, NP2 - 1) as i:
                for b in range(2):
                    sp.wait_ge(h_ready, i * 2 + b + 1)
                    sp.dma_start(xin[:, b, :], x_v[bass.ds(i * 2 + (b + 2), 1)].rearrange("o p d -> p (o d)")
                                 ).then_inc(x_in[b], 16)
            rows(0, 1)
            with sp.Fori(1, NK) as k:
                for e in range(2):
                    rows(k, e)
            sp.wait_ge(sr_ready, NJ)
            with nc.allow_non_contiguous_dma("s is turned from a column into a row"):
                sp.dma_start(s0_d.rearrange("o (j p) -> p (o j)", p=P),
                             sr[:, 0:NJ, 0:1].rearrange("p j o -> p (j o)")).then_inc(late_out, 16)
            sp.wait_ge(wh_ready, NT)
            sp.dma_start(wh_d[NT - 1], wh[:, 1, :]).then_inc(late_out, 16)
            sp.wait_ge(late_out, 32)

        @block.gpsimd
        def _(pool):
            nc.gpsimd.memset(ident[:, :], 0.0).then_inc(zeroed, 1)
            nc.gpsimd.memset(diagf, 0.0).then_inc(zeroed, 1)
            nc.gpsimd.memset(eps[:, :], EPS).then_inc(consts, 1)
            pool.wait_ge(zeroed, 2)
            nc.gpsimd.affine_select(out=ident[:, :], in_=ident[:, :], compare_op=ALU.not_equal, fill=1.0,
                                    base=0, pattern=[[-1, P]], channel_multiplier=1).then_inc(consts, 1)
            for e in range(2):
                nc.gpsimd.affine_select(out=diagf[:, e, :], in_=diagf[:, e, :], compare_op=ALU.not_equal,
                                        fill=float(ONE << (8 * e)), base=0, pattern=[[-1, P]],
                                        channel_multiplier=1).then_inc(consts, 1)
            pool.wait_ge(consts, 4)
            nc.gpsimd.tensor_copy(identb[:, :], ident[:, :]).then_inc(consts, 1)
            nc.gpsimd.tensor_copy(diag[:, :], diagf.rearrange("p e n -> p (e n)")).then_inc(consts, 1)

            with pool.Fori(0, NP2) as i:
                for b in range(2):
                    pool.wait_ge(own_ready, (i * 2 + b) * 2 + 2)
                    pool.dma_start(own_d[bass.ds(i * 2 + b, 1)].rearrange("o p d -> p (o d)"),
                                   ownA[:, b, :]).then_inc(own_out[b], 16)
            for b in range(2):
                pool.wait_ge(own_out[b], 16 * NP2)

            def keep(k, e):
                for f in range(2):
                    pool.wait_ge(words_copied, (k * 2 + e) * 2 + (f + 1))
                    hold(pool, waits_passed)
                    nc.gpsimd.tensor_copy(
                        mask32[:, f * HK:(f + 1) * HK, bass.ds((k * 2 + e) * (P // 2), P // 2)],
                        mT[:, e, f * HK * P:(f + 1) * HK * P].bitcast(I32).rearrange("p (k n) -> p k n", k=HK)
                    ).then_inc(kept, 1)

            def row(k, e):
                for dst, src in ((xt, x_v), (own, own_d)):
                    pool.dma_start(dst[:, e, :], src[bass.ds(k, 1), :, e * D:(e + 1) * D]
                                   .rearrange("o p d -> p (o d)")).then_inc(row_in[e], 16)

            def store_x1(k, e):
                pool.wait_ge(x1_ready, k * 2 + (e + 1))
                pool.dma_start(x1_d[bass.ds(k * 2 + e, 1)].rearrange("o p d -> p (o d)"), x1[:, e, :]
                               ).then_inc(x1_out[e], 16)

            def store_wh(t, e):
                pool.wait_ge(wh_ready, t + 1)
                pool.dma_start(wh_d[bass.ds(t, 1)].rearrange("o p d -> p (o d)"), wh[:, e, :]
                               ).then_inc(wh_out[e], 16)

            row(0, 0)
            row(0, 1)
            keep(0, 0)
            keep(0, 1)
            store_x1(0, 0)
            row(1, 0)
            with pool.Fori(1, NK - 1) as k:
                keep(k, 0)
                store_x1(k - 1, 1)
                row(k, 1)
                store_wh(k * 2 - 2, 0)
                keep(k, 1)
                store_x1(k, 0)
                row(k + 1, 0)
                store_wh(k * 2 - 1, 1)
            keep(NK - 1, 0)
            store_x1(NK - 2, 1)
            row(NK - 1, 1)
            store_wh(NT - 4, 0)
            keep(NK - 1, 1)
            store_x1(NK - 1, 0)
            store_wh(NT - 3, 1)
            store_x1(NK - 1, 1)
            store_wh(NT - 2, 0)
            for e in range(2):
                pool.wait_ge(x1_out[e], 16 * NK)
                pool.wait_ge(wh_out[e], 16 * (NK - e))

        @block.tensor
        def _(pe):
            pe.wait_ge(weights_in, 16 * 9)
            pe.wait_ge(consts, 4)
            for i in range(2):
                for c in range(2):
                    for q in range(2):
                        last = nc.tensor.transpose(ps_t32[i][:, (q * 2 + c) * P:(q * 2 + c + 1) * P],
                                                   w_in[i][:, c, q * P:(q + 1) * P], ident[:, :])
                last.then_inc(wT_ready, 1)
            for c in range(2):
                for i in range(2):
                    if c == 0:
                        pe.wait_ge(wT_copied, i + 1)
                    for q in range(2):
                        last = nc.tensor.matmul(ps_mm[c][:, i * D:(i + 1) * D],
                                                wT[i][:, q, c * P:(c + 1) * P], wc[:, 2 * i + q, :],
                                                start=(i == 0 and q == 0), stop=(q == 1),
                                                skip_group_check=True)
                last.then_inc(wmm_ready, 1)
            pe.wait_ge(bwide_ready, 1)
            for q in range(4):
                last = nc.tensor.matmul(ps_t32[0][:, 0:D], bwide[:, q, :], wc[:, q, :],
                                        start=(q == 0), stop=(q == 3))
            last.then_inc(wmm_ready, 1)

            def transposes(k, b):
                pe.wait_ge(h_ready, k + 1)
                pe.wait_ge(hT_copied, k + 1)
                for q in range(4):
                    last = nc.tensor.transpose(ps_hT[b][:, q * P:(q + 1) * P],
                                               h[:, b, q * P:(q + 1) * P], ident[:, :])
                last.then_inc(hT_ready, 1)

            def products(k, b, e):
                if e == 0:
                    pe.wait_ge(hT_copied, k + 3)
                    pe.wait_ge(mm_free, 2 * k + 2)
                for c in range(2):
                    for hp, wp in ((0, 0), (0, 1), (1, 0)):
                        last = nc.tensor.matmul(ps_mm[2 * b + e][:, :],
                                                hT[hp][:, b, (2 * e + c) * P:(2 * e + c + 1) * P],
                                                ab[wp][:, c, :], start=(c == 0 and hp + wp == 0),
                                                stop=(c == 1 and hp == 1))
                last.then_inc(mm_ready, 1)

            transposes(0, 0)
            transposes(1, 1)
            pe.wait_ge(ab_ready, 3)
            products(0, 0, 0)
            products(0, 0, 1)
            with pe.Fori(0, NP2 - 1) as i:
                for b in range(2):
                    products(i * 2 + (b + 1), 1 - b, 0)
                    transposes(i * 2 + (b + 2), b)
                    products(i * 2 + (b + 1), 1 - b, 1)
            products(NK - 1, 1, 0)
            products(NK - 1, 1, 1)

            def words(t, e):
                for f in range(2):
                    pe.wait_ge(bits_ready, t * 2 + (f + 1))
                    if not isinstance(t, int) or t >= 1:
                        pe.wait_ge(words_copied, t * 2 + (f - 1))
                    w = bits[:, f, :].bitcast(BF16)
                    for q in range(HK):
                        last = nc.tensor.transpose(ps_t[f][:, q * P:(q + 1) * P], w[:, q * P:(q + 1) * P],
                                                   identb[:, :])
                    last.then_inc(words_ready, 1)

            def sums(t, e, f):
                if f == 0:
                    pe.wait_ge(words_copied, t * 2 + 2)
                    if not isinstance(t, int) or t >= 2:
                        pe.wait_ge(x1_ready, t - 1)
                    hold(pe, waits_passed)
                m = mT[:, e, :].bitcast(F8).rearrange("p (k n b) -> p k b n", k=NK, b=2)
                for kk in range(f * HK, (f + 1) * HK):
                    for b in range(2):
                        last = nc.tensor.matmul(ps_a[e][:, :], m[:, kk, b, :], g[:, 2 * kk + b, :],
                                                start=(kk == 0 and b == 0), stop=(kk == NK - 1 and b == 1))
                if f == 1:
                    last.then_inc(agg_ready, 1)

            def turn_h1(t, e):
                pe.wait_ge(h1_ready, t + 1)
                if not isinstance(t, int) or t >= 1:
                    pe.wait_ge(h1T_copied, t)
                for c in range(2):
                    last = nc.tensor.transpose(ps_h[:, c * P:(c + 1) * P], h1[:, e, c * P:(c + 1) * P], ident[:, :])
                last.then_inc(h1T_ready, 1)

            def wh_product(t, e):
                pe.wait_ge(h1T_copied, t + 1)
                if not isinstance(t, int) or t >= 1:
                    pe.wait_ge(sr_ready, t)
                for c in range(2):
                    for hp, wp in ((0, 0), (0, 1), (1, 0)):
                        last = nc.tensor.matmul(ps_w[:, 0:E1], h1T[:, e, hp, c * P:(c + 1) * P],
                                                wext[:, wp, c, :], start=(c == 0 and hp + wp == 0),
                                                stop=(c == 1 and hp == 1))
                last.then_inc(wh_mm_ready, 1)

            def tile(t, e, first=False, final=False):
                sums(t, e, 0)
                if not final:
                    words(t + 1, 1 - e)
                if not first:
                    turn_h1(t - 1, 1 - e)
                sums(t, e, 1)
                if not first:
                    wh_product(t - 1, 1 - e)

            pe.wait_ge(consts, 6)
            words(0, 0)
            pe.wait_ge(mm_free, 2 * NK + 4)
            tile(0, 0, first=True)
            tile(1, 1)
            with pe.Fori(1, NK - 1) as k:
                for e in range(2):
                    tile(k * 2 + e, e)
            tile(NT - 2, 0)
            tile(NT - 1, 1, final=True)
            turn_h1(NT - 1, 1)
            wh_product(NT - 1, 1)

        @block.scalar
        def _(act):
            act.wait_ge(consts, 4)

            def stds(k):
                act.wait_ge(var_ready, k + 1)
                nc.scalar.activation(std, mv[:, :, 1], ACT.Sqrt, bias=eps[:, 0:1]).then_inc(std_ready, 1)

            def norm(k, b):
                act.wait_ge(norm_ready, k + 1)
                if not isinstance(k, int) or k >= 2:
                    act.wait_ge(hT_ready, k - 1)
                for e in range(2):
                    last = nc.scalar.activation(h[:, b, e * D:(e + 1) * D], xin[:, b, e * D:(e + 1) * D], ACT.Relu,
                                                bias=shift[:, e:e + 1], scale=rstd[:, e:e + 1])
                last.then_inc(h_ready, 1)

            def high_hT(k, b):
                act.wait_ge(hT_ready, k + 1)
                nc.scalar.activation(hT[0][:, b, :], ps_hT[b][:, :], ACT.Copy).then_inc(hT_high, 1)

            def highs(k, b):
                for e in range(2):
                    act.wait_ge(mm_ready, k * 2 + (e + 1))
                    nc.scalar.activation(g[:, bass.ds(k * 2 + e, 1), 0:D], ps_mm[2 * b + e][:, D:2 * D].unsqueeze(1),
                                         ACT.Copy, scale=GSCALE / WSCALE).then_inc(high_ready, 1)

            stds(0)
            norm(0, 0)
            for i in range(2):
                act.wait_ge(wT_ready, i + 1)
                nc.scalar.activation(wT[i].rearrange("p q d -> p (q d)"), ps_t32[i], ACT.Copy
                                     ).then_inc(wT_copied, 1)
            stds(1)
            norm(1, 1)
            for c in range(2):
                act.wait_ge(wmm_ready, c + 1)
                nc.scalar.activation(ab[0][:, c, :], ps_mm[c][:, :], ACT.Copy, scale=WSCALE).then_inc(ab_high, 1)
            high_hT(0, 0)
            high_hT(1, 1)
            act.wait_ge(wa_step, 8)
            nc.scalar.activation(wext[:, 0, :, :], w_raw, ACT.Copy, scale=WSCALE).then_inc(ab_high, 1)
            with act.Fori(0, NP2 - 1) as i:
                for b in range(2):
                    stds(i * 2 + (b + 2))
                    highs(i * 2 + b, b)
                    norm(i * 2 + (b + 2), b)
                    high_hT(i * 2 + (b + 2), b)
            highs(NK - 2, 0)
            highs(NK - 1, 1)

            def degrees(t):
                for f in range(2):
                    if not isinstance(t, int) or t or f:
                        act.wait_ge(deg_ready, t * 2 + f)
                    act.wait_ge(bits_ready, t * 2 + (f + 1))
                    nc.scalar.activation(junk[:, :], bits[:, f, :], ACT.Copy,
                                         accum_out=degp[:, bass.ds(t, 1), f:f + 1].rearrange("p o f -> p (o f)")
                                         ).then_inc(deg_ready, 1)

            def norm1(t, e):
                act.wait_ge(var1_ready, t + 1)
                nc.scalar.activation(std1[:, :], mv1[:, 1:2], ACT.Sqrt, bias=eps[:, 0:1]).then_inc(std1_ready, 1)
                act.wait_ge(norm1_ready, t + 1)
                if not isinstance(t, int) or t >= 2:
                    act.wait_ge(h1T_ready, t - 1)
                nc.scalar.activation(h1[:, e, :], x1[:, e, :], ACT.Relu, bias=shift1[:, 0:1], scale=rstd1[:, 0:1]
                                     ).then_inc(h1_ready, 1)

            def high_h1T(t, e):
                act.wait_ge(h1T_ready, t + 1)
                nc.scalar.activation(h1T[:, e, 0, :], ps_h[:, 0:D], ACT.Copy).then_inc(h1T_high, 1)

            def copy_wh(t, e, k):
                act.wait_ge(wh_mm_ready, t + 1)
                if not isinstance(k, int) or k:
                    act.wait_ge(wh_out[e], k * 16)
                nc.scalar.activation(wh[:, e, :], ps_w[:, 0:D], ACT.Copy, scale=VSCALE / WSCALE).then_inc(wh_ready, 1)
                nc.scalar.activation(sr[:, bass.ds(t, 1), :], ps_w[:, D:E1].unsqueeze(1), ACT.Copy,
                                     scale=1.0 / WSCALE).then_inc(sr_ready, 1)

            degrees(0)
            degrees(1)
            degrees(2)
            norm1(0, 0)
            high_h1T(0, 0)
            degrees(3)
            copy_wh(0, 0, 0)
            norm1(1, 1)

            def two_tiles(k):
                high_h1T(k * 2 - 1, 1)
                degrees(k * 2 + 2)
                copy_wh(k * 2 - 1, 1, k - 1)
                norm1(k * 2, 0)
                high_h1T(k * 2, 0)
                degrees(k * 2 + 3)
                copy_wh(k * 2, 0, k)
                norm1(k * 2 + 1, 1)

            two_tiles(1)
            with act.Fori(2, NK - 1) as k:
                two_tiles(k)
            high_h1T(NT - 3, 1)
            copy_wh(NT - 3, 1, NK - 2)
            norm1(NT - 2, 0)
            high_h1T(NT - 2, 0)
            copy_wh(NT - 2, 0, NK - 1)
            norm1(NT - 1, 1)
            high_h1T(NT - 1, 1)
            copy_wh(NT - 1, 1, NK - 1)

        @block.vector
        def _(dve):
            dve.sem_inc(hT_copied, 2)
            dve.sem_inc(mm_free, 4)

            def variances(k, b, i):
                dve.wait_ge(x_in[b], (i + 1) * 16)
                for e in range(2):
                    last = nc.vector.bn_stats(stats[:, e, :], xin[:, b, e * D:(e + 1) * D])
                last.then_inc(dve_step, 1)
                dve.wait_ge(dve_step, k * 2 + 1)
                if not isinstance(k, int) or k:
                    dve.wait_ge(h_ready, k)
                hold(dve, waits_passed)
                for e in range(2):
                    last = nc.vector.bn_aggr(mv[:, e, :], stats[:, e, :])
                last.then_inc(var_ready, 1)

            def factors(k):
                dve.wait_ge(std_ready, k + 1)
                nc.vector.reciprocal(rstd, std).then_inc(dve_step, 1)
                dve.wait_ge(dve_step, k * 2 + 2)
                nc.vector.scalar_tensor_tensor(shift, mv[:, :, 0], -1.0, rstd, ALU.mult, ALU.mult
                                               ).then_inc(norm_ready, 1)

            def low_hT(k, b):
                dve.wait_ge(hT_high, k + 1)
                nc.vector.tensor_tensor(hT[1][:, b, :], ps_hT[b][:, :], hT[0][:, b, :], ALU.subtract
                                        ).then_inc(hT_copied, 1)

            def outputs(k, b, i):
                if not isinstance(i, int) or i:
                    dve.wait_ge(own_out[b], i * 16)
                for e in range(2):
                    bank = ps_mm[2 * b + e]
                    dve.wait_ge(high_ready, k * 2 + (e + 1))
                    nc.vector.scalar_tensor_tensor(ownA[:, b, e * D:(e + 1) * D], bank[:, 0:D], 1.0 / WSCALE,
                                                   cbias, ALU.mult, ALU.add).then_inc(own_ready, 1)
                    nc.vector.scalar_tensor_tensor(g[:, bass.ds(k * 2 + e, 1), D:2 * D].rearrange("p o d -> p (o d)"),
                                                   bank[:, D:2 * D], GSCALE / WSCALE,
                                                   g[:, bass.ds(k * 2 + e, 1), 0:D].rearrange("p o d -> p (o d)"),
                                                   ALU.mult, ALU.subtract).then_inc(mm_free, 1)

            variances(0, 0, 0)
            factors(0)
            variances(1, 1, 0)
            factors(1)
            dve.wait_ge(weights_in, 16 * 9)
            nc.vector.tensor_copy(bwide, bcol.unsqueeze(2).to_broadcast([P, 4, P])).then_inc(bwide_ready, 1)
            n = 0
            for c in range(2):
                for i in range(2):
                    nc.vector.tensor_tensor(aprod, w_raw[:, c, 0:D], abc[:, i, :], ALU.mult).then_inc(wa_step, 1)
                    n += 1
                    dve.wait_ge(wa_step, n)
                    nc.vector.tensor_reduce(w_raw[:, c, D + H * i:D + H * (i + 1)],
                                            aprod.rearrange("p (h d) -> p h d", h=H), AX_X, ALU.add
                                            ).then_inc(wa_step, 1)
                    n += 1
                    dve.wait_ge(wa_step, n)
            for c in range(2):
                dve.wait_ge(ab_high, c + 1)
                nc.vector.scalar_tensor_tensor(ab[1][:, c, :], ps_mm[c][:, :], WSCALE, ab[0][:, c, :],
                                               ALU.mult, ALU.subtract).then_inc(ab_ready, 1)
            dve.wait_ge(wmm_ready, 3)
            nc.vector.tensor_tensor(cbias, ps_t32[0][:, 0:D], bcomb, ALU.add).then_inc(ab_ready, 1)
            low_hT(0, 0)
            dve.wait_ge(ab_high, 3)
            nc.vector.scalar_tensor_tensor(wext[:, 1, :, :], w_raw, WSCALE, wext[:, 0, :, :],
                                           ALU.mult, ALU.subtract).then_inc(ab_ready, 1)
            dve.wait_ge(ab_ready, 4)

            def two_pairs(i):
                for b in range(2):
                    variances(i * 2 + (b + 2), b, i + 1)
                    low_hT(i * 2 + (b + 1), 1 - b)
                    factors(i * 2 + (b + 2))
                    outputs(i * 2 + b, b, i)

            two_pairs(0)
            with dve.Fori(1, NP2 - 1) as i:
                two_pairs(i)

            def to_bits(t):
                for f in range(2):
                    dve.wait_ge(stage_in[f], (t + 1) * 16)
                    if not (isinstance(t, int) and t == 0):
                        dve.wait_ge(words_ready, t * 2 + (f - 1))
                        dve.wait_ge(deg_ready, t * 2 + (f - 1))
                    nc.vector.tensor_scalar(bits[:, f, :], stage[:, f, :], 0.0, float(ONE), ALU.is_gt, ALU.mult
                                            ).then_inc(bits_ready, 1)

            def copy_words(t, e):
                for f in range(2):
                    dve.wait_ge(words_ready, t * 2 + (f + 1))
                    if not isinstance(t, int) or t >= 2:
                        if f == 0:
                            dve.wait_ge(agg_ready, t - 1)
                        dve.wait_ge(kept, t * 2 + (f - 3))
                    nc.vector.tensor_copy(mT[:, e, f * HK * P:(f + 1) * HK * P], ps_t[f][:, :]
                                          ).then_inc(words_copied, 1)

            def post(t, e, k):
                STEPS = 7

                def link(ins, n):
                    ins.then_inc(post_step, 1)
                    dve.wait_ge(post_step, t * STEPS + n)

                dve.wait_ge(deg_ready, t * 2 + 2)
                link(nc.vector.tensor_reduce(deg[:, 0:1], degp[:, bass.ds(t, 1), :], AX_X, ALU.add), 1)
                link(nc.vector.tensor_scalar(deg[:, 1:2], deg[:, 0:1], float(ONE), GSCALE / ONE, ALU.max, ALU.mult), 2)
                link(nc.vector.reciprocal(deg[:, 2:3], deg[:, 1:2]), 3)
                dve.wait_ge(agg_ready, t + 1)
                dve.wait_ge(row_in[e], (k + 1) * 32)
                link(nc.vector.scalar_tensor_tensor(part[:, :], ps_a[e][:, 0:D], deg[:, 2:3], own[:, e, :],
                                                    ALU.mult, ALU.add), 4)
                link(nc.vector.scalar_tensor_tensor(part[:, :], ps_a[e][:, D:2 * D], deg[:, 2:3], part[:, :],
                                                    ALU.mult, ALU.add), 5)
                if not isinstance(t, int) or t >= 2:
                    dve.wait_ge(x1_out[e], k * 16)
                    dve.wait_ge(h1_ready, t - 1)
                nc.vector.scalar_tensor_tensor(x1[:, e, :], part[:, :], 0.0, xt[:, e, :], ALU.max, ALU.add
                                               ).then_inc(x1_ready, 1)
                dve.wait_ge(x1_ready, t + 1)
                link(nc.vector.bn_stats(stats1[:, :], x1[:, e, :]), 6)
                if not isinstance(t, int) or t >= 1:
                    dve.wait_ge(h1_ready, t)
                hold(dve, waits_passed)
                nc.vector.bn_aggr(mv1[:, :], stats1[:, :]).then_inc(var1_ready, 1)
                dve.wait_ge(std1_ready, t + 1)
                link(nc.vector.reciprocal(rstd1[:, :], std1[:, :]), 7)
                nc.vector.scalar_tensor_tensor(shift1[:, :], mv1[:, 0:1], -1.0, rstd1[:, :], ALU.mult, ALU.mult
                                               ).then_inc(norm1_ready, 1)

            def low_h1T(t, e):
                dve.wait_ge(h1T_high, t + 1)
                nc.vector.tensor_tensor(h1T[:, e, 1, :], ps_h[:, 0:D], h1T[:, e, 0, :], ALU.subtract
                                        ).then_inc(h1T_copied, 1)

            low_hT(NK - 1, 1)
            to_bits(0)
            outputs(NK - 2, 0, NP2 - 1)
            outputs(NK - 1, 1, NP2 - 1)
            copy_words(0, 0)
            to_bits(1)
            copy_words(1, 1)
            to_bits(2)
            post(0, 0, 0)
            copy_words(2, 0)
            low_h1T(0, 0)
            to_bits(3)
            post(1, 1, 0)
            with dve.Fori(1, NK - 1) as k:
                for e in range(2):
                    copy_words(k * 2 + (e + 1), 1 - e)
                    low_h1T(k * 2 + (e - 1), 1 - e)
                    to_bits(k * 2 + (e + 2))
                    post(k * 2 + e, e, k)
            copy_words(NT - 1, 1)
            low_h1T(NT - 3, 1)
            post(NT - 2, 0, NK - 1)
            low_h1T(NT - 2, 0)
            post(NT - 1, 1, NK - 1)
            low_h1T(NT - 1, 1)


def layer1(nc, x1_d, wh_d, s_d, s0_d, mask32, sr, diag, ident, out):
    x1_v = x1_d.rearrange("(s j) p (h d) -> s h p j d", j=NJ, h=H)
    wh_v = wh_d.rearrange("t p (h d) -> h p t d", h=H)
    out_v = out.rearrange("(s k p e) (h d) -> s h e p k d", s=NS, p=P, e=2, h=H)
    WS = STRIP // 2
    ASIGN = sum(not dve_has(k, b) for k in range(NK) for b in range(2))
    with ExitStack() as ctx:
        def sb(name, shape, dt):
            return ctx.enter_context(nc.sbuf_tensor(name, shape, dt))

        def sem(name):
            return ctx.enter_context(nc.semaphore(name))

        fac = sb("fac", [P, 4, H, NT], F32)
        rbias = sb("rbias", [P, 2, NG, NT], F32)
        srow = sb("srow", [P, 2, 1, STRIP], F32)
        sgn = sb("sgn", [P, 4, 2 * STRIP], I8)
        pos = sb("pos", [P, 4, WS], I32)
        neg = sb("neg", [P, 4, WS], I32)
        val = sb("val", [P, NT, 2 * VBLK], F16)
        whx = sb("whx", [P, NT, DV], F32)
        vtmp = sb("vtmp", [P, 2 * CH, DV], F32)
        total = sb("total", [P, NJ, VBLK], F32)
        num = sb("num", [P, NJ, DV], F32)
        den = sb("den", [P, 2, NJ], F32)
        y = sb("yout", [P, NJ, DK], F32)
        ylow = sb("ylow", [P, NJ, DK], F32)
        x1s = sb("x1s", [P, NJ, DK], F32)
        acc = [ctx.enter_context(nc.psum_tensor(f"acc{j}", [P, 512], F32)) for j in range(NJ)]

        spare = total[:, :, :].rearrange("p j n -> p (j n)")

        def by_head(at):
            return spare[:, at:at + H * NT].rearrange("p (h t) -> p h t", h=H)

        s_c, r_c, dr, y_c, bound = (by_head(i * H * NT) for i in range(5))
        ex = spare[:, 5 * H * NT:7 * H * NT].rearrange("p (i h t) -> p i h t", i=2, h=H)
        s_row = spare[:, 7 * H * NT:8 * H * NT]
        rmax = spare[:, 8 * H * NT:8 * H * NT + H]
        rall = spare[:, 8 * H * NT + H:8 * H * NT + 2 * H]
        ps_s = acc[NJ - 1][:, 0:P]

        rmax_ready = sem("rmax_ready")
        rall_ready = sem("rall_ready")
        s_compact = sem("s_compact")
        sT_ready = sem("sT_ready")
        s_row_ready = sem("s_row_ready")
        s_out = sem("s_out")
        step = sem("step2")
        expo_ready = sem("expo_ready")
        self_edges = sem("self_edges")
        rbias_ready = sem("rbias_ready")
        fac_ready = sem("fac_ready")
        waits_passed = sem("waits_passed3")
        ones_set = sem("ones_set")
        s_in = sem("s_in")
        first_wh_in = [sem(f"first_wh_in{i}") for i in range(2)]
        wh_in = sem("wh_in")
        x1_in = sem("x1_in")
        act_signs = sem("act_signs")
        dve_signs = sem("dve_signs")
        first_values = sem("first_values")
        neg_ready = sem("neg_ready")
        split_ready = sem("split_ready")
        pe_pair = sem("pe_pair")
        pe_bank = sem("pe_bank")
        val_step = sem("val_step")
        minus_ready = sem("minus_ready")
        plus_ready = sem("plus_ready")
        num_ready = sem("num_ready")
        den_step = sem("den_step")
        den_ready = sem("den_ready")
        y_step = sem("y_step")
        ylow_ready = sem("ylow_ready")
        exp_ready = sem("exp_ready")
        y_ready = sem("y_ready")
        stored = sem("stored")
        last_step = sem("last_step")
        block = ctx.enter_context(nc.Block())

        @block.sync
        def _(sp):
            def load_s(gr, slot):
                sp.dma_start(srow[:, bass.ds(slot, 1), :, :].rearrange("p a o n -> p (a o) n"),
                             s_d[bass.ds(gr, 1), :].partition_broadcast(P)).then_inc(s_in, 16)

            def load_x1(gr):
                sp.dma_start(x1s[:, :, :], x1_v[bass.ds(gr % NS, 1), bass.ds(gr // NS, 1)]
                             .rearrange("a b p j d -> p (a b j) d")).then_inc(x1_in, 16)

            def store(gr):
                sp.wait_ge(y_ready, gr + 1)
                for e in range(2):
                    sp.dma_start(out_v[bass.ds(gr % NS, 1), bass.ds(gr // NS, 1), e]
                                 .rearrange("a b p k d -> p (a b k) d"),
                                 y[:, :, :].rearrange("p (k e) d -> p e k d", e=2)[:, e]).then_inc(stored, 16)

            def next_s(gr):
                sp.wait_ge(act_signs, (gr + 1) * ASIGN)
                hold(sp, waits_passed)
                sp.wait_ge(dve_signs, (gr + 1) * (NT - ASIGN))
                sp.wait_ge(s_in, (gr + 2) * 16)
                load_s(gr + 2, gr % 2)

            sp.sem_inc(stored, 32)
            sp.dma_start(srow[:, 0, :, :].rearrange("p o n -> p (o n)"),
                         s0_d[0:1, :].partition_broadcast(P).rearrange("p o n -> p (o n)")).then_inc(s_in, 16)
            sp.wait_ge(s_row_ready, 1)
            sp.dma_start(s_d.rearrange("g (j p) -> (g j) p", p=P), s_row).then_inc(s_out, 16)
            sp.wait_ge(s_out, 16)
            sp.wait_ge(s_in, 16)
            load_s(1, 1)
            load_x1(0)
            next_s(0)
            with sp.Fori(1, NG - 2) as gr:
                store(gr - 1)
                load_x1(gr)
                next_s(gr)
            for gr in (NG - 2, NG - 1):
                store(gr - 1)
                load_x1(gr)
            store(NG - 1)
            sp.wait_ge(stored, 32 * (NG + 1))

        @block.gpsimd
        def _(pool):
            def load_wh(h):
                pool.dma_start(whx[:, :, 0:DK], wh_v[bass.ds(h, 1)].rearrange("o p t d -> p (o t) d")
                               ).then_inc(wh_in, 16)

            pool.sem_inc(num_ready, 1)
            pool.sem_inc(val_step, VSTEPS)
            pool.wait_ge(rmax_ready, 1)
            nc.gpsimd.partition_all_reduce(rall, rmax, P, bass.bass_isa.ReduceOp.max
                                           ).then_inc(rall_ready, 1)
            nc.gpsimd.memset(whx[:, :, DK:DV], VSCALE).then_inc(ones_set, 1)
            pool.wait_ge(ones_set, 1)
            pool.wait_ge(fac_ready, 1)

            def values(h, first, chunks):
                if first:
                    pool.wait_ge(first_wh_in[1], 16)
                else:
                    pool.wait_ge(wh_in, h * 16)
                for c in chunks:
                    if not first:
                        if c < NCH - 1:
                            pool.wait_ge(pe_pair, (h * NS - 1) * (NQ - 1) + (c + 1) * (CH // 2))
                        else:
                            pool.wait_ge(pe_bank, h * NS * NJ)
                    t0 = 2 * CH * c
                    for br in range(2):
                        n = (h * NCH + c) * VSTEPS + 3 * br
                        hi = val[:, t0:t0 + 2 * CH, br * VBLK:br * VBLK + DV]
                        lo = val[:, t0:t0 + 2 * CH, br * VBLK + DV:(br + 1) * VBLK]
                        f = fac[:, br, bass.ds(h, 1), t0:t0 + 2 * CH].rearrange("p o t -> p (o t)")
                        pool.wait_ge(val_step, n)
                        for dst in (vtmp[:, :, :], hi):
                            nc.gpsimd.tensor_tensor(dst, whx[:, t0:t0 + 2 * CH, :],
                                                    f.unsqueeze(2).to_broadcast([P, 2 * CH, DV]), ALU.mult
                                                    ).then_inc(val_step, 1)
                        pool.wait_ge(val_step, n + 2)
                        nc.gpsimd.tensor_tensor(lo, vtmp[:, :, :], hi, ALU.subtract).then_inc(val_step, 1)

            def sums(gr):
                pool.wait_ge(plus_ready, gr * NJ + 2 * NJ)
                nc.gpsimd.tensor_tensor(num[:, :, :], total[:, :, 0:DV], total[:, :, DV:VBLK], ALU.add
                                        ).then_inc(num_ready, 1)

            YS = 3

            def divide(gr):
                pool.wait_ge(num_ready, gr + 2)
                pool.wait_ge(den_ready, gr + 1)
                pool.wait_ge(stored, (gr + 1) * 32)
                nc.gpsimd.tensor_tensor(y[:, :, :], num[:, :, 0:DK],
                                        den[:, 1, :].unsqueeze(2).to_broadcast([P, NJ, DK]), ALU.mult
                                        ).then_inc(y_step, 1)
                pool.wait_ge(y_step, gr * YS + 1)
                hold(pool, waits_passed)
                nc.gpsimd.tensor_scalar(ylow[:, :, :], y[:, :, :], 0.0, None, ALU.min).then_inc(ylow_ready, 1)

            def finish(gr):
                pool.wait_ge(ylow_ready, gr + 1)
                hold(pool, waits_passed)
                nc.gpsimd.tensor_scalar(y[:, :, :], y[:, :, :], 0.0, -1.0, ALU.max, ALU.add).then_inc(y_step, 1)
                pool.wait_ge(y_step, gr * YS + 2)
                pool.wait_ge(exp_ready, gr + 1)
                nc.gpsimd.tensor_tensor(y[:, :, :], y[:, :, :], ylow[:, :, :], ALU.add).then_inc(y_step, 1)
                pool.wait_ge(y_step, gr * YS + 3)
                pool.wait_ge(x1_in, (gr + 1) * 16)
                nc.gpsimd.tensor_tensor(y[:, :, :], y[:, :, :], x1s[:, :, :], ALU.add).then_inc(y_ready, 1)

            values(0, True, range(1, NCH))
            with pool.Fori(0, H - 1) as h:
                pool.wait_ge(val_step, (h + 1) * (NCH * VSTEPS))
                pool.wait_ge(first_values, VSTEPS)
                load_wh(h + 1)
                with pool.Fori(0, NS - 1) as s:
                    sums(h * NS + s)
                    divide(h * NS + s)
                    finish(h * NS + s)
                values(h + 1, False, range(NCH - 2))
                sums(h * NS + (NS - 1))
                values(h + 1, False, range(NCH - 2, NCH - 1))
                divide(h * NS + (NS - 1))
                values(h + 1, False, range(NCH - 1, NCH))
                finish(h * NS + (NS - 1))
            with pool.Fori(0, NS - 1) as s:
                sums(s + (H - 1) * NS)
                divide(s + (H - 1) * NS)
                finish(s + (H - 1) * NS)

        @block.tensor
        def _(pe):
            pe.wait_ge(s_compact, 1)
            nc.tensor.transpose(ps_s, s_c.rearrange("p h t -> p (h t)"), ident[:, :]).then_inc(sT_ready, 1)
            pe.wait_ge(s_row_ready, 1)
            pe.wait_ge(first_values, VSTEPS)

            def bytes_of(t):
                return t.bitcast(F8).rearrange("p (n b) -> p b n", b=2)

            with pe.Fori(0, NG) as gr:
                for k in range(NK):
                    if k % CH == 0:
                        pe.wait_ge(val_step, gr // NS * (NCH * VSTEPS) + (k // CH + 1) * VSTEPS)
                    if k % 2 == 0 or k == 3:
                        pe.wait_ge(split_ready, gr * SPLITS + splits(k // 2, k % 2))
                        hold(pe, waits_passed)
                    for j in range(NJ):
                        if k == 0:
                            pe.wait_ge(minus_ready, gr * NJ + (j + 1))
                            pe.wait_ge(plus_ready, gr * NJ + (j + 1))
                            hold(pe, waits_passed)
                        for b in range(2):
                            first = k == 0 and b == 0
                            final = k == NK - 1 and b == 1
                            for br, m in enumerate((pos, neg)):
                                last = nc.tensor.matmul(
                                    acc[j][:, br * VBLK:(br + 1) * VBLK],
                                    bytes_of(m[:, k % 4, j * (P // 2):(j + 1) * (P // 2)])[:, b, :],
                                    val[:, 2 * k + b, br * VBLK:(br + 1) * VBLK],
                                    start=first and br == 0, stop=final, skip_group_check=True)
                        if k == NK - 1:
                            last.then_inc(pe_bank, 1)
                    if k % 2 == 1 and k < NK - 1:
                        last.then_inc(pe_pair, 1)

        @block.scalar
        def _(act):
            act.wait_ge(sT_ready, 1)
            nc.scalar.activation(s_row, ps_s, ACT.Copy).then_inc(s_row_ready, 1)
            for i, (t0, t1) in enumerate(((0, 2 * CH), (2 * CH, NT))):
                act.dma_start(whx[:, t0:t1, 0:DK], wh_v[0, :, t0:t1, :]).then_inc(first_wh_in[i], 16)
            act.wait_ge(expo_ready, 1)
            nc.scalar.activation(fac[:, 0, :, :], dr, ACT.Exp)
            nc.scalar.activation(fac[:, 1, :, :], dr, ACT.Exp, scale=SLOPE)
            nc.scalar.activation(fac[:, 2:4, :, :], ex, ACT.Exp).then_inc(fac_ready, 1)
            act.wait_ge(rbias_ready, 1)
            act.wait_ge(fac_ready, 1)

            act.sem_inc(minus_ready, NJ)

            def sign(gr, k, b):
                if not (isinstance(gr, int) and k < 4):
                    act.wait_ge(neg_ready, gr * SPLITS + (splits(k // 2 - 2, k % 2) if k >= 4 else k // 2 - 1))
                nc.scalar.activation(sign_bytes(sgn, k, b), srow[:, bass.ds(gr % 2, 1), 0, :].rearrange("p o n -> p (o n)"),
                                     ACT.Sign, bias=rbias[:, 0, bass.ds(gr, 1), 2 * k + b]).then_inc(act_signs, 1)

            def read_minus(gr):
                for j in range(NJ):
                    act.wait_ge(pe_bank, gr * NJ + (j + 1))
                    if j == 0:
                        act.wait_ge(num_ready, gr + 1)
                    nc.scalar.activation(total[:, j, :], acc[j][:, VBLK:2 * VBLK], ACT.Copy,
                                         scale=fac_col(fac, 3, gr, j)).then_inc(minus_ready, 1)

            def group(gr, first):
                act.wait_ge(s_in, (gr + 1) * 16)
                for k in range(NK):
                    for b in range(2):
                        if not dve_has(k, b):
                            sign(gr, k, b)
                    if k == 3 and not first:
                        read_minus(gr - 1)
                    if k == 13 and not first:
                        act.wait_ge(ylow_ready, gr)
                        nc.scalar.activation(ylow[:, :, :], ylow[:, :, :], ACT.Exp).then_inc(exp_ready, 1)

            group(0, True)
            with act.Fori(1, NG) as gr:
                group(gr, False)
            read_minus(NG - 1)
            act.wait_ge(ylow_ready, NG)
            nc.scalar.activation(ylow[:, :, :], ylow[:, :, :], ACT.Exp).then_inc(exp_ready, 1)

        @block.vector
        def _(dve):
            n = 0

            def link(ins):
                nonlocal n
                n += 1
                ins.then_inc(step, 1)
                dve.wait_ge(step, n)

            nc.vector.tensor_reduce(rmax, sr[:, :, H:2 * H].rearrange("p t h -> p h t"), AX_X, ALU.max
                                    ).then_inc(rmax_ready, 1)
            nc.vector.tensor_copy(s_c, sr[:, :, 0:H].rearrange("p t h -> p h t")).then_inc(s_compact, 1)
            link(nc.vector.tensor_copy(r_c, sr[:, :, H:2 * H].rearrange("p t h -> p h t")))
            for h in range(H):
                for i, sign in enumerate((1.0, -1.0)):
                    last = nc.vector.tensor_scalar(rbias[:, i, h * NS:(h + 1) * NS, :],
                                                   r_c[:, h, :].unsqueeze(1).to_broadcast([P, NS, NT]),
                                                   sign, None, ALU.mult)
            last.then_inc(rbias_ready, 1)
            dve.wait_ge(rall_ready, 1)
            dve.wait_ge(s_compact, 1)
            for h in range(H):
                nc.vector.tensor_scalar(dr[:, h, :], r_c[:, h, :], rall[:, h:h + 1], None, ALU.subtract)
                last = nc.vector.tensor_scalar(y_c[:, h, :], s_c[:, h, :], rall[:, h:h + 1], None, ALU.add)
            link(last)
            link(nc.vector.scalar_tensor_tensor(bound, y_c, SLOPE, y_c, ALU.mult, ALU.max))
            nc.vector.tensor_tensor(ex[:, 0], y_c, bound, ALU.subtract)
            nc.vector.scalar_tensor_tensor(ex[:, 1], y_c, SLOPE, bound, ALU.mult, ALU.subtract
                                           ).then_inc(expo_ready, 1)

            def set_self_edges(q):
                for k in (2 * q, 2 * q + 1):
                    blk = mask32[:, k, k * P:(k + 1) * P]
                    last = nc.vector.tensor_tensor(blk, blk, diag[:, :].bitcast(I32), ALU.bitwise_or)
                last.then_inc(self_edges, 1)

            set_self_edges(0)

            dve.wait_ge(first_wh_in[0], 16)
            dve.wait_ge(ones_set, 1)
            dve.wait_ge(fac_ready, 1)
            vtmp0 = num[:, :, :]
            for br in range(2):
                hi = val[:, 0:2 * CH, br * VBLK:br * VBLK + DV]
                lo = val[:, 0:2 * CH, br * VBLK + DV:(br + 1) * VBLK]
                nc.vector.tensor_tensor(vtmp0, whx[:, 0:2 * CH, :],
                                        fac[:, br, 0, 0:2 * CH].unsqueeze(2).to_broadcast([P, 2 * CH, DV]),
                                        ALU.mult).then_inc(first_values, 1)
                dve.wait_ge(first_values, 3 * br + 1)
                nc.vector.tensor_copy(hi, vtmp0).then_inc(first_values, 1)
                dve.wait_ge(first_values, 3 * br + 2)
                nc.vector.tensor_tensor(lo, vtmp0, hi, ALU.subtract).then_inc(first_values, 1)
                dve.wait_ge(first_values, 3 * br + 3)
            dve.wait_ge(rbias_ready, 1)
            dve.sem_inc(plus_ready, NJ)

            def signs(gr, q):
                for k in (2 * q, 2 * q + 1):
                    if dve_has(k, 1):
                        nc.vector.tensor_scalar(sign_bytes(sgn, k, 1),
                                                srow[:, bass.ds(gr % 2, 1), 0, :].rearrange("p o n -> p (o n)"),
                                                rbias[:, 1, bass.ds(gr, 1), 2 * k + 1], float(ONE), ALU.is_lt,
                                                ALU.mult).then_inc(dve_signs, 1)

            def split(gr, q, first, between):
                dve.wait_ge(dve_signs, gr * (NT - ASIGN)
                            + sum(dve_has(i, b) for i in range(2 * q + 2) for b in range(2)))
                dve.wait_ge(act_signs, gr * ASIGN + sum(not dve_has(i, b) for i in range(2 * q + 2) for b in range(2)))
                if q >= 2:
                    dve.wait_ge(pe_pair, gr * (NQ - 1) + (q - 1))
                elif not first and q == 0:
                    dve.wait_ge(pe_pair, gr * (NQ - 1))
                elif not first:
                    dve.wait_ge(pe_bank, gr * NJ)
                for i, (k0, k1) in enumerate(((2, 3), (3, 4)) if q == 1 else ((2 * q, 2 * q + 2),)):
                    slot = k0 % 4
                    n = k1 - k0
                    m = mask32[:, k0:k1, bass.ds((gr % NS) * WS, WS)]
                    sg = sgn[:, slot:slot + n, :].bitcast(I32)
                    nc.vector.tensor_tensor(neg[:, slot:slot + n, :], sg, m, ALU.bitwise_and).then_inc(neg_ready, 1)
                    if between and k1 == 2 * q + 2:
                        signs(gr, q + 1)
                    dve.wait_ge(neg_ready, gr * SPLITS + splits(q, i))
                    nc.vector.tensor_tensor(pos[:, slot:slot + n, :], neg[:, slot:slot + n, :], m, ALU.bitwise_xor
                                            ).then_inc(split_ready, 1)

            def read_plus(gr):
                for j in range(NJ):
                    dve.wait_ge(minus_ready, gr * NJ + (NJ + j + 1))
                    nc.vector.scalar_tensor_tensor(total[:, j, :], acc[j][:, 0:VBLK], fac_col(fac, 2, gr, j),
                                                   total[:, j, :], ALU.mult, ALU.add).then_inc(plus_ready, 1)

            def denominators(gr):
                dve.wait_ge(num_ready, gr + 2)
                nc.vector.tensor_scalar(den[:, 0, :], num[:, :, DK], 1e-30, None, ALU.max).then_inc(den_step, 1)
                dve.wait_ge(den_step, gr + 1)
                nc.vector.reciprocal(den[:, 1, :], den[:, 0, :]).then_inc(den_ready, 1)

            def group(gr, first):
                dve.wait_ge(s_in, (gr + 1) * 16)
                signs(gr, 0)
                if not first:
                    signs(gr, 1)
                for q in range(NQ):
                    if q == 1 and not first:
                        read_plus(gr - 1)
                    if first:
                        dve.wait_ge(self_edges, q + 1)
                    split(gr, q, first, (q > 0 or first) and q not in (3, NQ - 1))
                    if q == 3:
                        signs(gr, 4)
                    if first and q < NQ - 1:
                        set_self_edges(q + 1)
                    if q == 2 and not first:
                        denominators(gr - 1)

            group(0, True)
            with dve.Fori(1, NG) as gr:
                group(gr, False)
            read_plus(NG - 1)

            def link_last(ins, n):
                ins.then_inc(last_step, 1)
                dve.wait_ge(last_step, n)

            dve.wait_ge(plus_ready, (NG + 1) * NJ)
            link_last(nc.vector.tensor_tensor(num[:, :, :], total[:, :, 0:DV], total[:, :, DV:VBLK], ALU.add), 1)
            link_last(nc.vector.tensor_scalar(den[:, 0, :], num[:, :, DK], 1e-30, None, ALU.max), 2)
            link_last(nc.vector.reciprocal(den[:, 1, :], den[:, 0, :]), 3)
            dve.wait_ge(stored, NG * 32)
            link_last(nc.vector.tensor_tensor(y[:, :, :], num[:, :, 0:DK],
                                              den[:, 1, :].unsqueeze(2).to_broadcast([P, NJ, DK]), ALU.mult), 4)
            nc.vector.tensor_scalar(ylow[:, :, :], y[:, :, :], 0.0, None, ALU.min).then_inc(ylow_ready, 1)
            dve.wait_ge(x1_in, NG * 16)
            link_last(nc.vector.scalar_tensor_tensor(y[:, :, :], y[:, :, :], 0.0, x1s[:, :, :], ALU.max, ALU.add), 5)
            dve.wait_ge(exp_ready, NG)
            nc.vector.scalar_tensor_tensor(y[:, :, :], ylow[:, :, :], -1.0, y[:, :, :], ALU.add, ALU.add
                                           ).then_inc(y_ready, 1)


def splits(q, i=0):
    return q + 1 + (1 if q > 1 else i)


SPLITS = splits(NQ - 1)


def hold(eng, waits_passed):
    eng.sem_inc(waits_passed, 1)


def dve_has(k, b):
    return b == 1 and k % 2 == 1 and k // 2 != 3


def sign_bytes(sgn, k, b):
    return sgn[:, k % 4, :].rearrange("p (n b) -> p b n", b=2)[:, b, :]


def fac_col(fac, i, gr, j):
    return fac[:, i, :, :].rearrange("p h t -> p (h t)")[:, bass.ds(gr * NJ + j, 1)]


_INS = ["x", "adj", "L0_gnn_W_self", "L0_gnn_b_self", "L0_gnn_W_nb", "L0_gnn_b_nb", "L0_gnn_W_comb",
        "L0_gnn_b_comb", "L1_gnn_W", "L1_gnn_a_l", "L1_gnn_a_r"]


def kernel(**inputs):
    import numpy as _np
    import concourse.bacc as _bacc
    from concourse import mybir as _mybir
    from concourse.bass_utils import run_bass_kernel_spmd as _run

    nc = _bacc.Bacc("TRN2", target_bir_lowering=False, num_devices=1)
    arrays, args = {}, []
    for name in _INS:
        a = _np.ascontiguousarray(inputs[name])
        arrays[f"in_{name}"] = a
        args.append(nc.dram_tensor(f"in_{name}", a.shape, _mybir.dt.from_np(a.dtype), kind="ExternalInput").ap())
    out = nc.dram_tensor("out", (N, D), F32, kind="ExternalOutput").ap()
    build(nc, *args, out)
    r = _run(nc, [arrays], core_ids=[0])
    return r.results[0]["out"]
```
